# Optimizing a Trainium2 kernel written in Bass

```python
import numpy as np
import jax
import jax.numpy as jnp

def _softmax(x, axis=-1):
    return jax.nn.softmax(x, axis=axis)

def _gelu(x):
    return jax.nn.gelu(x, approximate=True)

def _silu(x):
    return jax.nn.silu(x)

def _sigmoid(x):
    return jax.nn.sigmoid(x)

def _layernorm(x, axis=-1, eps=1e-05):
    m = jnp.mean(x, axis=axis, keepdims=True)
    v = jnp.var(x, axis=axis, keepdims=True)
    return (x - m) / jnp.sqrt(v + eps)

def _scatter_add(tgt, idx, src, axis=0):
    return tgt.at[idx].add(src)

def _segment_sum(src, seg, n):
    return jax.ops.segment_sum(src, seg, n)
kernel_name = 'mk_dlrm_tower_d1_rec_r8_26ed45'

def setup_inputs(seed: int=0):
    np.random.seed(seed)
    _w = jnp.asarray

    def _rec_inputs():
        import jax
        import jax.numpy as jnp
        _tk = jax.random.key(seed)
        dense_ctx = jax.random.normal(jax.random.fold_in(_tk, 190), (512, 16), jnp.float32)
        ids = jnp.stack([jax.random.randint(jax.random.fold_in(_tk, 200 + f), (512,), 0, v, jnp.int32) for f, v in enumerate([1000, 125000, 1250, 125000, 1250, 125000, 12500, 1000, 1000, 12500, 125000, 1000, 1000, 12500, 125000, 12500, 125000, 12500, 12500, 125000, 1000, 1000, 12500, 1250, 1000, 12500, 1250, 1000, 125000, 1250, 125000, 1250, 125000, 12500, 1250, 1250, 1250, 125000, 1250])], axis=1)
        tbl_0 = 0.05 * jax.random.normal(jax.random.fold_in(_tk, 500 + 0), (1000, 16), jnp.float32)
        tbl_1 = 0.05 * jax.random.normal(jax.random.fold_in(_tk, 500 + 1), (125000, 16), jnp.float32)
        tbl_2 = 0.05 * jax.random.normal(jax.random.fold_in(_tk, 500 + 2), (1250, 16), jnp.float32)
        tbl_3 = 0.05 * jax.random.normal(jax.random.fold_in(_tk, 500 + 3), (125000, 16), jnp.float32)
        tbl_4 = 0.05 * jax.random.normal(jax.random.fold_in(_tk, 500 + 4), (1250, 16), jnp.float32)
        tbl_5 = 0.05 * jax.random.normal(jax.random.fold_in(_tk, 500 + 5), (125000, 16), jnp.float32)
        tbl_6 = 0.05 * jax.random.normal(jax.random.fold_in(_tk, 500 + 6), (12500, 16), jnp.float32)
        tbl_7 = 0.05 * jax.random.normal(jax.random.fold_in(_tk, 500 + 7), (1000, 16), jnp.float32)
        tbl_8 = 0.05 * jax.random.normal(jax.random.fold_in(_tk, 500 + 8), (1000, 16), jnp.float32)
        tbl_9 = 0.05 * jax.random.normal(jax.random.fold_in(_tk, 500 + 9), (12500, 16), jnp.float32)
        tbl_10 = 0.05 * jax.random.normal(jax.random.fold_in(_tk, 500 + 10), (125000, 16), jnp.float32)
        tbl_11 = 0.05 * jax.random.normal(jax.random.fold_in(_tk, 500 + 11), (1000, 16), jnp.float32)
        tbl_12 = 0.05 * jax.random.normal(jax.random.fold_in(_tk, 500 + 12), (1000, 16), jnp.float32)
        tbl_13 = 0.05 * jax.random.normal(jax.random.fold_in(_tk, 500 + 13), (12500, 16), jnp.float32)
        tbl_14 = 0.05 * jax.random.normal(jax.random.fold_in(_tk, 500 + 14), (125000, 16), jnp.float32)
        tbl_15 = 0.05 * jax.random.normal(jax.random.fold_in(_tk, 500 + 15), (12500, 16), jnp.float32)
        tbl_16 = 0.05 * jax.random.normal(jax.random.fold_in(_tk, 500 + 16), (125000, 16), jnp.float32)
        tbl_17 = 0.05 * jax.random.normal(jax.random.fold_in(_tk, 500 + 17), (12500, 16), jnp.float32)
        tbl_18 = 0.05 * jax.random.normal(jax.random.fold_in(_tk, 500 + 18), (12500, 16), jnp.float32)
        tbl_19 = 0.05 * jax.random.normal(jax.random.fold_in(_tk, 500 + 19), (125000, 16), jnp.float32)
        tbl_20 = 0.05 * jax.random.normal(jax.random.fold_in(_tk, 500 + 20), (1000, 16), jnp.float32)
        tbl_21 = 0.05 * jax.random.normal(jax.random.fold_in(_tk, 500 + 21), (1000, 16), jnp.float32)
        tbl_22 = 0.05 * jax.random.normal(jax.random.fold_in(_tk, 500 + 22), (12500, 16), jnp.float32)
        tbl_23 = 0.05 * jax.random.normal(jax.random.fold_in(_tk, 500 + 23), (1250, 16), jnp.float32)
        tbl_24 = 0.05 * jax.random.normal(jax.random.fold_in(_tk, 500 + 24), (1000, 16), jnp.float32)
        tbl_25 = 0.05 * jax.random.normal(jax.random.fold_in(_tk, 500 + 25), (12500, 16), jnp.float32)
        tbl_26 = 0.05 * jax.random.normal(jax.random.fold_in(_tk, 500 + 26), (1250, 16), jnp.float32)
        tbl_27 = 0.05 * jax.random.normal(jax.random.fold_in(_tk, 500 + 27), (1000, 16), jnp.float32)
        tbl_28 = 0.05 * jax.random.normal(jax.random.fold_in(_tk, 500 + 28), (125000, 16), jnp.float32)
        tbl_29 = 0.05 * jax.random.normal(jax.random.fold_in(_tk, 500 + 29), (1250, 16), jnp.float32)
        tbl_30 = 0.05 * jax.random.normal(jax.random.fold_in(_tk, 500 + 30), (125000, 16), jnp.float32)
        tbl_31 = 0.05 * jax.random.normal(jax.random.fold_in(_tk, 500 + 31), (1250, 16), jnp.float32)
        tbl_32 = 0.05 * jax.random.normal(jax.random.fold_in(_tk, 500 + 32), (125000, 16), jnp.float32)
        tbl_33 = 0.05 * jax.random.normal(jax.random.fold_in(_tk, 500 + 33), (12500, 16), jnp.float32)
        tbl_34 = 0.05 * jax.random.normal(jax.random.fold_in(_tk, 500 + 34), (1250, 16), jnp.float32)
        tbl_35 = 0.05 * jax.random.normal(jax.random.fold_in(_tk, 500 + 35), (1250, 16), jnp.float32)
        tbl_36 = 0.05 * jax.random.normal(jax.random.fold_in(_tk, 500 + 36), (1250, 16), jnp.float32)
        tbl_37 = 0.05 * jax.random.normal(jax.random.fold_in(_tk, 500 + 37), (125000, 16), jnp.float32)
        tbl_38 = 0.05 * jax.random.normal(jax.random.fold_in(_tk, 500 + 38), (1250, 16), jnp.float32)
        _rk = jax.random.fold_in(_tk, 7)
        W_top1 = 0.0606339 * jax.random.normal(jax.random.fold_in(_tk, 801), (272, 512), jnp.float32)
        W_top2 = 0.0441942 * jax.random.normal(jax.random.fold_in(_tk, 802), (512, 256), jnp.float32)
        W_top3 = 0.0625 * jax.random.normal(jax.random.fold_in(_tk, 803), (256, 1), jnp.float32)
        b_top1 = jnp.zeros((512,), jnp.float32)
        b_top2 = jnp.zeros((256,), jnp.float32)
        return (dense_ctx, ids, tbl_0, tbl_1, tbl_2, tbl_3, tbl_4, tbl_5, tbl_6, tbl_7, tbl_8, tbl_9, tbl_10, tbl_11, tbl_12, tbl_13, tbl_14, tbl_15, tbl_16, tbl_17, tbl_18, tbl_19, tbl_20, tbl_21, tbl_22, tbl_23, tbl_24, tbl_25, tbl_26, tbl_27, tbl_28, tbl_29, tbl_30, tbl_31, tbl_32, tbl_33, tbl_34, tbl_35, tbl_36, tbl_37, tbl_38, W_top1, b_top1, W_top2, b_top2, W_top3)
    dense_ctx, ids, tbl_0, tbl_1, tbl_2, tbl_3, tbl_4, tbl_5, tbl_6, tbl_7, tbl_8, tbl_9, tbl_10, tbl_11, tbl_12, tbl_13, tbl_14, tbl_15, tbl_16, tbl_17, tbl_18, tbl_19, tbl_20, tbl_21, tbl_22, tbl_23, tbl_24, tbl_25, tbl_26, tbl_27, tbl_28, tbl_29, tbl_30, tbl_31, tbl_32, tbl_33, tbl_34, tbl_35, tbl_36, tbl_37, tbl_38, W_top1, b_top1, W_top2, b_top2, W_top3 = _rec_inputs()

    def _L0_rec_setup():
        import jax, jax.numpy as jnp
        import numpy as np
        F0 = 39
        CIN_SIZES = [128, 128, 128]
        B, D = (512, 16)

        def _cin_forward(x, weights, biases):
            x0 = x
            xk = x
            fields = [F0] + CIN_SIZES
            outs = []
            for idx, s in enumerate(CIN_SIZES):
                fk = fields[idx]
                w = weights[idx].reshape(F0, fk, s)
                out = jnp.einsum('bid,bjd,ijs->bsd', x0, xk, w) + biases[idx][None, :, None]
                outs.append(out)
                xk = out
            res = jnp.concatenate(outs[1:], axis=1)
            return jnp.sum(res, axis=-1)
        key = jax.random.key(seed)
        ks = jax.random.split(key, 7)
        fields = [F0] + CIN_SIZES
        inp = {'x': jax.random.normal(ks[0], (B, F0, D), dtype=jnp.float32)}
        for i, s in enumerate(CIN_SIZES):
            m = fields[i] * F0
            inp[f'w{i}'] = jax.random.normal(ks[1 + 2 * i], (m, s), dtype=jnp.float32) * (2.0 / (m + s)) ** 0.5
            inp[f'b{i}'] = jax.random.normal(ks[2 + 2 * i], (s,), dtype=jnp.float32) * 0.02
        return inp
    _L0_rec_all = _L0_rec_setup()
    _L0_rec_in = {k: v for k, v in _L0_rec_all.items() if k in ('w0', 'b0', 'w1', 'b1', 'w2', 'b2')}
    del _L0_rec_all
    return {'dense_ctx': dense_ctx, 'ids': ids, 'tbl_0': tbl_0, 'tbl_1': tbl_1, 'tbl_2': tbl_2, 'tbl_3': tbl_3, 'tbl_4': tbl_4, 'tbl_5': tbl_5, 'tbl_6': tbl_6, 'tbl_7': tbl_7, 'tbl_8': tbl_8, 'tbl_9': tbl_9, 'tbl_10': tbl_10, 'tbl_11': tbl_11, 'tbl_12': tbl_12, 'tbl_13': tbl_13, 'tbl_14': tbl_14, 'tbl_15': tbl_15, 'tbl_16': tbl_16, 'tbl_17': tbl_17, 'tbl_18': tbl_18, 'tbl_19': tbl_19, 'tbl_20': tbl_20, 'tbl_21': tbl_21, 'tbl_22': tbl_22, 'tbl_23': tbl_23, 'tbl_24': tbl_24, 'tbl_25': tbl_25, 'tbl_26': tbl_26, 'tbl_27': tbl_27, 'tbl_28': tbl_28, 'tbl_29': tbl_29, 'tbl_30': tbl_30, 'tbl_31': tbl_31, 'tbl_32': tbl_32, 'tbl_33': tbl_33, 'tbl_34': tbl_34, 'tbl_35': tbl_35, 'tbl_36': tbl_36, 'tbl_37': tbl_37, 'tbl_38': tbl_38, 'W_top1': W_top1, 'b_top1': b_top1, 'W_top2': W_top2, 'b_top2': b_top2, 'W_top3': W_top3, 'L0_rec_w0': _L0_rec_in['w0'], 'L0_rec_b0': _L0_rec_in['b0'], 'L0_rec_w1': _L0_rec_in['w1'], 'L0_rec_b1': _L0_rec_in['b1'], 'L0_rec_w2': _L0_rec_in['w2'], 'L0_rec_b2': _L0_rec_in['b2']}

def reference(dense_ctx, ids, tbl_0, tbl_1, tbl_2, tbl_3, tbl_4, tbl_5, tbl_6, tbl_7, tbl_8, tbl_9, tbl_10, tbl_11, tbl_12, tbl_13, tbl_14, tbl_15, tbl_16, tbl_17, tbl_18, tbl_19, tbl_20, tbl_21, tbl_22, tbl_23, tbl_24, tbl_25, tbl_26, tbl_27, tbl_28, tbl_29, tbl_30, tbl_31, tbl_32, tbl_33, tbl_34, tbl_35, tbl_36, tbl_37, tbl_38, W_top1, b_top1, W_top2, b_top2, W_top3, L0_rec_w0, L0_rec_b0, L0_rec_w1, L0_rec_b1, L0_rec_w2, L0_rec_b2):
    import jax
    import jax.numpy as jnp

    def _L0_rec_ref(x, w0, b0, w1, b1, w2, b2):
        import jax, jax.numpy as jnp
        import numpy as np
        F0 = 39
        CIN_SIZES = [128, 128, 128]
        B, D = (512, 16)

        def _cin_forward(x, weights, biases):
            x0 = x
            xk = x
            fields = [F0] + CIN_SIZES
            outs = []
            for idx, s in enumerate(CIN_SIZES):
                fk = fields[idx]
                w = weights[idx].reshape(F0, fk, s)
                out = jnp.einsum('bid,bjd,ijs->bsd', x0, xk, w) + biases[idx][None, :, None]
                outs.append(out)
                xk = out
            res = jnp.concatenate(outs[1:], axis=1)
            return jnp.sum(res, axis=-1)
        return _cin_forward(x, [w0, w1, w2], [b0, b1, b2])
    e = jnp.stack([tbl_0[ids[:, 0]], tbl_1[ids[:, 1]], tbl_2[ids[:, 2]], tbl_3[ids[:, 3]], tbl_4[ids[:, 4]], tbl_5[ids[:, 5]], tbl_6[ids[:, 6]], tbl_7[ids[:, 7]], tbl_8[ids[:, 8]], tbl_9[ids[:, 9]], tbl_10[ids[:, 10]], tbl_11[ids[:, 11]], tbl_12[ids[:, 12]], tbl_13[ids[:, 13]], tbl_14[ids[:, 14]], tbl_15[ids[:, 15]], tbl_16[ids[:, 16]], tbl_17[ids[:, 17]], tbl_18[ids[:, 18]], tbl_19[ids[:, 19]], tbl_20[ids[:, 20]], tbl_21[ids[:, 21]], tbl_22[ids[:, 22]], tbl_23[ids[:, 23]], tbl_24[ids[:, 24]], tbl_25[ids[:, 25]], tbl_26[ids[:, 26]], tbl_27[ids[:, 27]], tbl_28[ids[:, 28]], tbl_29[ids[:, 29]], tbl_30[ids[:, 30]], tbl_31[ids[:, 31]], tbl_32[ids[:, 32]], tbl_33[ids[:, 33]], tbl_34[ids[:, 34]], tbl_35[ids[:, 35]], tbl_36[ids[:, 36]], tbl_37[ids[:, 37]], tbl_38[ids[:, 38]]], axis=1)
    z = _L0_rec_ref(e, L0_rec_w0, L0_rec_b0, L0_rec_w1, L0_rec_b1, L0_rec_w2, L0_rec_b2)
    z = z.reshape(z.shape[0], -1)
    h = jnp.concatenate([z, dense_ctx], axis=1)
    h = jnp.maximum(h @ W_top1 + b_top1, 0.0)
    h = jnp.maximum(h @ W_top2 + b_top2, 0.0)
    y = h @ W_top3
    return y

_drawn_inputs = setup_inputs


def setup_inputs(seed=0):
    import zlib

    import numpy as np

    out = dict(_drawn_inputs(seed))
    spreads = {'b_top1': (0.0, 0.8), 'b_top2': (0.0, 0.639)}
    factors = {'tbl_0': 8.0,
     'tbl_1': 8.0,
     'tbl_2': 8.0,
     'tbl_3': 8.0,
     'tbl_4': 8.0,
     'tbl_5': 8.0,
     'tbl_6': 8.0,
     'tbl_7': 8.0,
     'tbl_8': 8.0,
     'tbl_9': 8.0,
     'tbl_10': 8.0,
     'tbl_11': 8.0,
     'tbl_12': 8.0,
     'tbl_13': 8.0,
     'tbl_14': 8.0,
     'tbl_15': 8.0,
     'tbl_16': 8.0,
     'tbl_17': 8.0,
     'tbl_18': 8.0,
     'tbl_19': 8.0,
     'tbl_20': 8.0,
     'tbl_21': 8.0,
     'tbl_22': 8.0,
     'tbl_23': 8.0,
     'tbl_24': 8.0,
     'tbl_25': 8.0,
     'tbl_26': 8.0,
     'tbl_27': 8.0,
     'tbl_28': 8.0,
     'tbl_29': 8.0,
     'tbl_30': 8.0,
     'tbl_31': 8.0,
     'tbl_32': 8.0,
     'tbl_33': 8.0,
     'tbl_34': 8.0,
     'tbl_35': 8.0,
     'tbl_36': 8.0,
     'tbl_37': 8.0,
     'tbl_38': 8.0,
     'L0_rec_w0': 8.0,
     'L0_rec_b0': 3.158,
     'L0_rec_w1': 3.452,
     'L0_rec_w2': 2.911,
     'dense_ctx': 3.344,
     'L0_rec_b1': 3.634,
     'L0_rec_b2': 3.942}
    for name, (base, spread) in spreads.items():
        noise = np.random.default_rng([zlib.crc32(name.encode()), seed]).standard_normal(out[name].shape)
        drawn = base * np.exp(spread * noise) if base else spread * noise
        out[name] = jnp.asarray(drawn.astype(out[name].dtype))
    for name, factor in factors.items():
        out[name] = (out[name] * factor).astype(out[name].dtype)
    return out
```

```python
from contextlib import ExitStack

import numpy as np

import concourse.bass as bass
import concourse.mybir as mybir

F32 = mybir.dt.float32
F32R = mybir.dt.float32r
I32 = mybir.dt.int32
ALU = mybir.AluOpType
ACT = mybir.ActivationFunctionType

P = 128
FIELDS = 39
D = 16
ROWS = 512
S = 128
BLOCK_ROWS = P
BLOCKS = ROWS // BLOCK_ROWS
BLOCK_TOKENS = BLOCK_ROWS * D
TILE = P
TILE_ROWS = TILE // D
TILES = BLOCK_TOKENS // TILE
GROUP_TILES = 4
GROUP = GROUP_TILES * TILE
GROUPS = TILES // GROUP_TILES
SHIFTS = (FIELDS + 1) // 2
CHUNK_SHIFTS = 3
CHUNK_ROWS = CHUNK_SHIFTS * FIELDS
FULL_CHUNKS = (SHIFTS - 2) // CHUNK_SHIFTS
CHUNKS = FULL_CHUNKS + 1
LAST_ROWS = 2 * FIELDS
SCRATCH_ROWS = FIELDS + SHIFTS - 1
BANK_FIELDS = 4
BANKS = (FIELDS + BANK_FIELDS - 1) // BANK_FIELDS
RING = BANKS // 2
HALF = BANKS // 2
G_COLS = (FIELDS + 1) * TILE_ROWS
TOP1, TOP2 = 512, 256
CTX = 16

GATHERS_A_TILE = 4
TURN_TILE = 11
ROUND_D = 4
ROUNDS = D // ROUND_D
SPLITS = 4
SPLIT_COLS = FIELDS * S // SPLITS
VSTEPS = HALF * BANK_FIELDS
STEPS = HALF + 1
LOAD_DMAS = 7
STORE_DMAS = 2


def fields_of(bank):
    return range(BANK_FIELDS * bank, min(BANK_FIELDS * (bank + 1), FIELDS))


def dlrm_tower(nc, a, out):
    ctx = ExitStack()
    with ctx:
        def sb(name, shape, dt=F32):
            return ctx.enter_context(nc.sbuf_tensor(name, shape, dt))

        def pb(name):
            return ctx.enter_context(nc.psum_tensor(name, [P, 512], F32))

        def sem(name):
            return ctx.enter_context(nc.semaphore(name))

        ident = sb("ident", [P, P])
        ids_all = sb("ids_all", [P, BLOCKS * FIELDS], I32)
        ids_block = sb("ids_block", [P, FIELDS], I32)
        w0_pair = sb("w0_pair", [CHUNK_ROWS, CHUNKS, S])
        w0_swap = sb("w0_swap", [CHUNK_ROWS, CHUNKS, S])
        w1_high = sb("w1_high", [P, FIELDS * S], F32R)
        w1_low = sb("w1_low", [P, FIELDS * S], F32R)
        w2 = sb("w2", [P, FIELDS * S])
        w_top1 = sb("w_top1", [P, 2, TOP1])
        w_top1c = sb("w_top1c", [CTX, TOP1])
        w_top2 = sb("w_top2", [P, TOP1 // P, TOP2])
        w_top3 = sb("w_top3", [P, TOP2 // P])
        b0 = sb("b0", [P, 1])
        b1_row = sb("b1_row", [P, S])
        b2 = sb("b2", [P, 1])
        b2_sum = sb("b2_sum", [P, 1])
        b_top1 = sb("b_top1", [P, TOP1 // P])
        b_top2 = sb("b_top2", [P, TOP2 // P])
        ctx_t = sb("ctx_t", [CTX, ROWS])
        row_mask = sb("row_mask", [P, TILE_ROWS])
        emb = sb("emb", [P, FIELDS * D])
        x0_fields = sb("x0_fields", [FIELDS, BLOCK_TOKENS])
        x0_tokens = sb("x0_tokens", [P, TILES, FIELDS])
        scratch = nc.dram_tensor("x0_scratch", (SCRATCH_ROWS, BLOCK_TOKENS), F32, kind="Internal").ap()
        pairs = [sb(f"pairs{n}", [CHUNK_ROWS, CHUNKS, GROUP]) for n in range(2)]
        firsts = [sb(f"firsts{n}", [CHUNK_ROWS, GROUP]) for n in range(2)]
        x1_high = [sb(f"x1_high{n}", [P, GROUP], F32R) for n in range(2)]
        x1_low = [sb(f"x1_low{n}", [P, GROUP], F32R) for n in range(2)]
        vec_sum = [[sb(f"vec_sum{n}{m}", [P, S]) for m in range(2)] for n in range(2)]
        scaled = [sb(f"scaled{n}", [P, BANK_FIELDS * S]) for n in range(HALF)]
        pool_sum = sb("pool_sum", [P, BANK_FIELDS * S])
        pool_fold = sb("pool_fold", [P, 2 * S])
        pool_out = sb("pool_out", [P, S])
        x2 = sb("x2", [P, S])
        spread = [sb(f"spread{n}", [P, G_COLS]) for n in range(2)]
        g_block = sb("g_block", [P, FIELDS + 1, BLOCK_ROWS])
        z1 = sb("z1", [P, ROWS])
        z2 = sb("z2", [P, ROWS])
        h1 = sb("h1", [P, TOP1 // P, ROWS])
        h2 = sb("h2", [P, TOP2 // P, ROWS])
        y_sb = sb("y_sb", [1, ROWS])
        warm = sb("warm", [P, 1])

        bank = [pb(f"bank{n}") for n in range(RING)]
        x1_ps = pb("x1_ps")
        turn_ps = pb("turn_ps")
        g_ps = pb("g_ps")
        z2_cols = g_ps[:, G_COLS:G_COLS + BLOCK_ROWS]

        s_ids = sem("ids_loaded")
        s_early = sem("early_weights_loaded")
        s_w1 = sem("w1_loaded")
        s_late = sem("late_weights_loaded")
        s_w2 = sem("w2_loaded")
        s_gather = sem("gathered")
        s_store = sem("x0_stored")
        s_load = [sem(f"operands_loaded{n}") for n in range(2)]
        s_out = sem("out_stored")
        s_idsb = sem("ids_block_ready")
        s_w0 = sem("w0_summed")
        s_w1h = sem("w1_high_ready")
        s_w1l = sem("w1_low_ready")
        s_b2 = sem("b2_summed")
        s_mask = sem("spread_masks_ready")
        s_turned = sem("fields_in_psum")
        s_fields = sem("x0_fields_ready")
        s_tturned = sem("tokens_in_psum")
        s_tokens = sem("x0_tokens_ready")
        s_prod = sem("products_ready")
        s_l0 = sem("layer0_done")
        s_x1h = sem("x1_high_ready")
        s_x1l = sem("x1_low_ready")
        s_y = sem("bank_filled")
        s_vstep = sem("vector_steps")
        s_abank = sem("scalar_bank_scaled")
        s_pstep = sem("pool_steps")
        s_comb = sem("halves_summed")
        s_x2 = sem("x2_ready")
        s_spread = sem("spread_ready")
        s_g = sem("g_in_psum")
        s_gsb = sem("g_block_written")
        s_z2 = sem("z2_in_psum")
        s_z = sem("z_written")
        s_z1 = sem("z1_written")
        s_m1 = sem("top1_in_psum")
        s_h1 = sem("h1_ready")
        s_m2 = sem("top2_in_psum")
        s_h2 = sem("h2_ready")
        s_m3 = sem("top3_in_psum")
        s_ysb = sem("y_ready")

        EARLY, LATE = 6, 10

        tables = [a[f"tbl_{f}"] for f in range(FIELDS)]
        emb_v = emb[:, :].rearrange("p (f d) -> p f d", d=D)
        x0_by_d = x0_fields[:, :].rearrange("f (b d) -> f d b", d=D)

        block = ctx.enter_context(nc.Block())

        def blocks(eng, body):
            with eng.Fori(0, BLOCKS - 1) as n:
                body(n, True)
            body(BLOCKS - 1, False)

        @block.sync
        def _(sp):
            sp.dma_start(ids_all[:, :], a["ids"]).then_inc(s_ids, 16)
            sp.dma_start(ident[:, :], a["ident"]).then_inc(s_early, 16)
            sp.dma_start(w0_pair[:, 0:FULL_CHUNKS, :], a["w0_pair"]).then_inc(s_early, 16)
            sp.dma_start(w0_swap[:, 0:FULL_CHUNKS, :], a["w0_swap"]).then_inc(s_early, 16)
            sp.dma_start(w0_pair[0:LAST_ROWS, FULL_CHUNKS, :], a["w0_pair_last"]).then_inc(s_early, 16)
            sp.dma_start(w0_swap[0:FIELDS, FULL_CHUNKS, :], a["w0_swap_last"]).then_inc(s_early, 16)
            sp.dma_start(b0[:, :], a["b0"]).then_inc(s_early, 16)
            sp.dma_start(w2[:, :], a["w1"]).then_inc(s_w1, 16)
            sp.dma_start(b1_row[:, :], a["b1"].to_broadcast([P, S])).then_inc(s_late, 16)
            sp.dma_start(b2[:, :], a["b2"]).then_inc(s_late, 16)
            sp.dma_start(row_mask[:, :], a["row_mask"]).then_inc(s_late, 16)
            sp.dma_start(w_top1[:, :, :], a["w_top1"]).then_inc(s_late, 16)
            sp.dma_start(w_top1c[:, :], a["w_top1c"]).then_inc(s_late, 16)
            sp.dma_start(w_top2[:, :, :], a["w_top2"]).then_inc(s_late, 16)
            sp.dma_start(w_top3[:, :], a["w_top3"]).then_inc(s_late, 16)
            sp.dma_start(b_top1[:, :], a["b_top1"]).then_inc(s_late, 16)
            sp.dma_start(b_top2[:, :], a["b_top2"]).then_inc(s_late, 16)
            sp.dma_start(ctx_t[:, :], a["ctx_t"]).then_inc(s_late, 16)

            def load_group(g):
                cols = slice(GROUP * g, GROUP * (g + 1))
                for c in range(CHUNK_SHIFTS):
                    rows = slice(FIELDS * c, FIELDS * (c + 1))
                    sp.dma_start(firsts[g % 2][rows, :], scratch[0:FIELDS, cols]).then_inc(s_load[g % 2], 16)
                    n = CHUNKS if c == 0 else FULL_CHUNKS
                    src = bass.AP(scratch.tensor, (c + 1) * BLOCK_TOKENS + GROUP * g,
                                  [[BLOCK_TOKENS, FIELDS], [CHUNK_SHIFTS * BLOCK_TOKENS, n], [1, GROUP]])
                    sp.dma_start(pairs[g % 2][rows, 0:n, :], src).then_inc(s_load[g % 2], 16)
                sp.dma_start(pairs[g % 2][FIELDS:LAST_ROWS, FULL_CHUNKS, :],
                             scratch[0:FIELDS, cols]).then_inc(s_load[g % 2], 16)

            def store_block(n):
                sp.wait_ge(s_fields, n * 4 + 4)
                sp.dma_start(scratch[0:FIELDS, :], x0_fields[:, :]).then_inc(s_store, 16)
                sp.dma_start(scratch[FIELDS:SCRATCH_ROWS, :],
                             x0_fields[0:SCRATCH_ROWS - FIELDS, :]).then_inc(s_store, 16)

            def first_group(n):
                sp.wait_ge(s_store, n * (16 * STORE_DMAS) + 16 * STORE_DMAS)
                load_group(0)

            store_block(0)
            first_group(0)
            sp.wait_ge(s_w1l, 4)
            sp.dma_start(w2[:, :], a["w2"]).then_inc(s_w2, 16)

            def body(n, more):
                for g in range(1, GROUPS):
                    sp.wait_ge(s_l0, n * GROUPS + (g - 1) + 1)
                    load_group(g)
                if more:
                    for buf in range(2):
                        sp.wait_ge(s_load[buf], (n + 1) * (16 * LOAD_DMAS * GROUPS // 2))
                    store_block(n + 1)
                    sp.wait_ge(s_l0, n * GROUPS + (GROUPS - 1) + 1)
                    first_group(n + 1)

            blocks(sp, body)
            sp.wait_ge(s_ysb, 1)
            sp.dma_start(out, y_sb[:, :]).then_inc(s_out, 16)
            sp.wait_ge(s_out, 16)

        @block.gpsimd
        def _(pool):
            pool.wait_ge(s_ids, 16)

            def take_ids(n):
                nc.gpsimd.tensor_copy(ids_block[:, :], ids_all[:, bass.ds(n * FIELDS, FIELDS)])\
                    .then_inc(s_idsb, 1)

            def gather(f):
                nc.gpsimd.indirect_dma_start(
                    emb[:, f * D:(f + 1) * D], None, tables[f],
                    bass.IndirectOffsetOnAxis(ap=ids_block[:, f:f + 1], axis=0)).then_inc(s_gather, 16)

            take_ids(0)
            pool.wait_ge(s_idsb, 1)
            for f in range(FIELDS):
                gather(f)
            nc.gpsimd.memset(pool_sum[:, :], 0.0).then_inc(s_pstep, STEPS)

            def sums(n, t):
                u = n * TILES + t
                done = u * STEPS + STEPS
                for q in range(1, HALF):
                    w = len(fields_of(2 * q + 1)) * S
                    pool.wait_ge(s_abank, u * HALF + (HALF + q + 1))
                    pool.wait_ge(s_pstep, done + (q - 1))
                    nc.gpsimd.tensor_tensor(pool_sum[:, 0:w], (scaled[0] if q == 1 else pool_sum)[:, 0:w],
                                            scaled[q][:, 0:w], ALU.add).then_inc(s_pstep, 1)
                pool.wait_ge(s_pstep, done + (HALF - 1))
                nc.gpsimd.tensor_tensor(pool_fold[:, :], pool_sum[:, 0:2 * S], pool_sum[:, 2 * S:4 * S],
                                        ALU.add).then_inc(s_pstep, 1)
                pool.wait_ge(s_pstep, done + HALF)
                pool.wait_ge(s_x2, u + 1 + 1)
                nc.gpsimd.tensor_tensor(pool_out[:, :], pool_fold[:, 0:S], pool_fold[:, S:2 * S],
                                        ALU.add).then_inc(s_pstep, 1)

            def body(n, more):
                if more:
                    pool.wait_ge(s_gather, (n + 1) * (16 * FIELDS))
                    take_ids(n + 1)
                for t in range(TILES):
                    if more and t == 0:
                        pool.wait_ge(s_idsb, n + 2)
                        pool.wait_ge(s_turned, (n + 1) * ROUNDS)
                    sums(n, t)
                    if more and t * GATHERS_A_TILE < FIELDS:
                        for f in range(t * GATHERS_A_TILE, min((t + 1) * GATHERS_A_TILE, FIELDS)):
                            gather(f)

            blocks(pool, body)

        @block.tensor
        def _(pe):
            def turn_fields(n, r):
                ps = turn_ps if r % 2 == 0 else x1_ps
                for c in range(ROUND_D):
                    mm = nc.tensor.transpose(ps[0:FIELDS, P * c:P * (c + 1)],
                                             emb_v[:, :, ROUND_D * r + c], ident[:, :])
                mm.then_inc(s_turned, 1)

            def turn_tokens(n, h):
                for c in range(TILES // 2):
                    t = h * (TILES // 2) + c
                    mm = nc.tensor.transpose(turn_ps[:, FIELDS * c:FIELDS * (c + 1)],
                                             x0_fields[:, TILE * t:TILE * (t + 1)],
                                             ident[0:FIELDS, 0:FIELDS])
                mm.then_inc(s_tturned, 1)

            def layer0(n, g):
                q = n * GROUPS + g
                pe.wait_ge(s_prod, q + 1)
                for c in range(CHUNKS):
                    k = CHUNK_ROWS if c < FULL_CHUNKS else LAST_ROWS
                    mm = nc.tensor.matmul(x1_ps[:, :], w0_pair[0:k, c, :], pairs[g % 2][0:k, c, :],
                                          start=(c == 0), stop=(c == CHUNKS - 1))
                mm.then_inc(s_l0, 1)

            def layer1(n, t):
                u = n * TILES + t
                if t % GROUP_TILES == 0:
                    q = n * GROUPS + t // GROUP_TILES
                    pe.wait_ge(s_x1h, q + 1)
                    pe.wait_ge(s_x1l, q + 1)
                g = t // GROUP_TILES
                cols = slice(TILE * (t % GROUP_TILES), TILE * (t % GROUP_TILES + 1))
                high, low = x1_high[g % 2][:, cols], x1_low[g % 2][:, cols]
                for k in range(BANKS):
                    before, back = (k - RING, 0) if k >= RING else (k + RING, 1)
                    if before % 2 == 0:
                        pe.wait_ge(s_vstep, u * VSTEPS + VSTEPS * (1 - back)
                                   + BANK_FIELDS * (before // 2 + 1))
                    else:
                        pe.wait_ge(s_abank, u * HALF + HALF * (1 - back) + (before // 2 + 1))
                    w = len(fields_of(k)) * S
                    ws = slice(BANK_FIELDS * S * k, BANK_FIELDS * S * k + w)
                    ps = bank[k % RING][:, 0:w]
                    nc.tensor.matmul(ps, high, w1_high[:, ws], start=True, stop=False)
                    nc.tensor.matmul(ps, high, w1_low[:, ws], start=False, stop=False)
                    nc.tensor.matmul(ps, low, w1_high[:, ws], start=False, stop=True).then_inc(s_y, 1)

            def sum_coordinates(n, t):
                u = n * TILES + t
                pe.wait_ge(s_x2, u + 2 + 1)
                pe.wait_ge(s_spread, u + 1 + 1)
                pe.wait_ge(s_gsb, u + 1)
                nc.tensor.matmul(g_ps[:, 0:G_COLS], x2[:, :], spread[t % 2][:, :],
                                 start=True, stop=True).then_inc(s_g, 1)

            def layer2(n):
                pe.wait_ge(s_gsb, (n + 1) * TILES + 1)
                pe.wait_ge(s_z, n + 1)
                pe.wait_ge(s_w2, 16)
                for i in range(FIELDS):
                    mm = nc.tensor.matmul(z2_cols, w2[:, S * i:S * (i + 1)], g_block[:, i, :],
                                          start=(i == 0), stop=(i == FIELDS - 1))
                mm.then_inc(s_z2, 1)

            for s in (s_y, s_g, s_l0, s_z2):
                pe.sem_inc(s, 1)
            pe.wait_ge(s_early, 16 * EARLY)
            pe.wait_ge(s_gather, 16 * FIELDS)
            for r in range(ROUNDS):
                if r >= 2:
                    pe.wait_ge(s_fields, r - 1)
                turn_fields(0, r)
            pe.wait_ge(s_fields, ROUNDS)
            turn_tokens(0, 0)
            pe.wait_ge(s_w0, 2)
            layer0(0, 0)
            pe.wait_ge(s_w1h, SPLITS)
            pe.wait_ge(s_w1l, SPLITS)

            def body(n, more):
                for t in range(TILES):
                    layer1(n, t)
                    if t == 1:
                        pe.wait_ge(s_tokens, n * 2 + 1)
                    if more and t == TURN_TILE:
                        pe.wait_ge(s_gather, (n + 2) * (16 * FIELDS))
                        pe.wait_ge(s_tokens, n * 2 + 2)
                        pe.wait_ge(s_x1l, (n + 1) * GROUPS)
                    if more and t == TURN_TILE + 1:
                        pe.wait_ge(s_fields, (n + 1) * ROUNDS + 2)
                    if more and t == TURN_TILE + 2:
                        pe.wait_ge(s_fields, (n + 2) * ROUNDS)
                    if t >= 1:
                        sum_coordinates(n, t - 1)
                    if t == 1:
                        turn_tokens(n, 1)
                    g = t // GROUP_TILES
                    if t % GROUP_TILES == 2 and g + 1 < GROUPS:
                        pe.wait_ge(s_x1l, n * GROUPS + (g + 1))
                        if g == 0:
                            pe.wait_ge(s_x1h, n * GROUPS + (g + 1))
                        layer0(n, g + 1)
                    if more and t == TURN_TILE:
                        turn_fields(n + 1, 0)
                        turn_fields(n + 1, 1)
                    if more and t == TURN_TILE + 1:
                        turn_fields(n + 1, 2)
                        turn_fields(n + 1, 3)
                    if more and t == TURN_TILE + 2:
                        turn_tokens(n + 1, 0)
                if more:
                    layer0(n + 1, 0)
                sum_coordinates(n, TILES - 1)
                layer2(n)

            blocks(pe, body)

            pe.wait_ge(s_late, 16 * LATE)
            pe.wait_ge(s_z1, BLOCKS + 1)
            pe.wait_ge(s_z, BLOCKS + 1)
            for m in range(TOP1 // P):
                ms = slice(P * m, P * (m + 1))
                nc.tensor.matmul(bank[m][:, :], w_top1c[:, ms], ctx_t[:, :], start=True, stop=False)
                nc.tensor.matmul(bank[m][:, :], w_top1[:, 0, ms], z1[:, :], start=False, stop=False)
                nc.tensor.matmul(bank[m][:, :], w_top1[:, 1, ms], z2[:, :], start=False,
                                 stop=True).then_inc(s_m1, 1)
            for c in range(TOP1 // P):
                pe.wait_ge(s_h1, c + 1)
                for m in range(TOP2 // P):
                    mm = nc.tensor.matmul((bank[4], x1_ps)[m][:, :], w_top2[:, c, P * m:P * (m + 1)],
                                          h1[:, c, :], start=(c == 0), stop=(c == TOP1 // P - 1))
                    if c == TOP1 // P - 1:
                        mm.then_inc(s_m2, 1)
            for c in range(TOP2 // P):
                pe.wait_ge(s_h2, c + 1)
                mm = nc.tensor.matmul(turn_ps[0:1, :], w_top3[:, c:c + 1], h2[:, c, :],
                                      start=(c == 0), stop=(c == TOP2 // P - 1))
            mm.then_inc(s_m3, 1)

        @block.scalar
        def _(act):
            act.wait_ge(s_w1, 16)
            for c in range(SPLITS):
                cs = slice(SPLIT_COLS * c, SPLIT_COLS * (c + 1))
                nc.scalar.copy(w1_high[:, cs], w2[:, cs]).then_inc(s_w1h, 1)
            act.wait_ge(s_late, 16 * LATE)
            nc.scalar.mul(b2_sum[:, :], b2[:, :], float(D)).then_inc(s_b2, 1)

            def take_fields(n, r):
                act.wait_ge(s_turned, n * ROUNDS + (r + 1))
                ps = turn_ps if r % 2 == 0 else x1_ps
                nc.scalar.copy(x0_by_d[:, ROUND_D * r:ROUND_D * (r + 1), :],
                               ps[0:FIELDS, :].rearrange("f (d b) -> f d b", b=P)).then_inc(s_fields, 1)

            def take_tokens(n, h):
                act.wait_ge(s_tturned, n * 2 + (h + 1))
                nc.scalar.copy(x0_tokens[:, h * (TILES // 2):(h + 1) * (TILES // 2), :],
                               turn_ps[:, 0:FIELDS * (TILES // 2)].rearrange("p (t f) -> p t f", f=FIELDS))\
                    .then_inc(s_tokens, 1)

            def take_x1_high(n, g):
                act.wait_ge(s_l0, n * GROUPS + (g + 1) + 1)
                nc.scalar.activation(x1_high[g % 2][:, :], x1_ps[:, :], ACT.Identity, bias=b0[:, 0:1])\
                    .then_inc(s_x1h, 1)

            def scale_banks(n, t):
                u = n * TILES + t
                for q in range(HALF):
                    k = 2 * q + 1
                    act.wait_ge(s_y, u * BANKS + (k + 1) + 1)
                    act.wait_ge(s_pstep, u * STEPS + max(q, 1))
                    for r, i in enumerate(fields_of(k)):
                        ins = nc.scalar.activation(scaled[q][:, S * r:S * (r + 1)],
                                                   bank[k % RING][:, S * r:S * (r + 1)], ACT.Copy,
                                                   scale=x0_tokens[:, t, i:i + 1])
                    ins.then_inc(s_abank, 1)

            def take_g(n, t):
                u = n * TILES + t
                act.wait_ge(s_g, u + 1 + 1)
                if t == 0:
                    act.wait_ge(s_z2, n + 1)
                    act.wait_ge(s_z1, n + 1)
                nc.scalar.copy(g_block[:, :, TILE_ROWS * t:TILE_ROWS * (t + 1)],
                               g_ps[:, 0:G_COLS].rearrange("p (i b) -> p i b", b=TILE_ROWS))\
                    .then_inc(s_gsb, 1)

            for s in (s_gsb, s_z, s_z1):
                act.sem_inc(s, 1)
            nc.scalar.copy(warm[:, :], b2[:, :]).then_inc(s_abank, HALF)
            for r in range(ROUNDS):
                take_fields(0, r)
            take_tokens(0, 0)
            act.wait_ge(s_early, 16 * EARLY)
            take_x1_high(0, 0)
            act.wait_ge(s_tokens, 1)

            def body(n, more):
                for t in range(TILES):
                    if t == TILES // 2:
                        act.wait_ge(s_tokens, n * 2 + 2)
                    scale_banks(n, t)
                    if t >= 1:
                        take_g(n, t - 1)
                    if t == 1:
                        act.wait_ge(s_spread, n * TILES + 1)
                        act.wait_ge(s_abank, n * (TILES * HALF) + HALF)
                        take_tokens(n, 1)
                    g = t // GROUP_TILES
                    if t % GROUP_TILES == 2 and g + 1 < GROUPS:
                        act.wait_ge(s_y, n * (BANKS * TILES) + g * BANKS * GROUP_TILES + 1)
                        take_x1_high(n, g + 1)
                    if more and t == TURN_TILE:
                        act.wait_ge(s_store, (n + 1) * (16 * STORE_DMAS))
                        act.wait_ge(s_tturned, n * 2 + 2)
                        take_fields(n + 1, 0)
                        take_fields(n + 1, 1)
                    if more and t == TURN_TILE + 1:
                        take_fields(n + 1, 2)
                        take_fields(n + 1, 3)
                    if more and t == TURN_TILE + 2:
                        act.wait_ge(s_spread, n * TILES + TILES // 2 + 1)
                        act.wait_ge(s_abank, n * (TILES * HALF) + HALF * (TILES // 2 + 1))
                        take_tokens(n + 1, 0)
                if more:
                    act.wait_ge(s_y, n * (BANKS * TILES) + (GROUPS - 1) * BANKS * GROUP_TILES + 1)
                    take_x1_high(n + 1, 0)
                take_g(n, TILES - 1)
                act.wait_ge(s_gsb, (n + 1) * TILES + 1)
                nc.scalar.copy(z1[:, bass.ds(n * BLOCK_ROWS, BLOCK_ROWS)], g_block[:, FIELDS, :])\
                    .then_inc(s_z1, 1)
                act.wait_ge(s_z2, n + 1 + 1)
                nc.scalar.activation(z2[:, bass.ds(n * BLOCK_ROWS, BLOCK_ROWS)], z2_cols, ACT.Identity,
                                     bias=b2_sum[:, 0:1]).then_inc(s_z, 1)
                if more:
                    act.wait_ge(s_tokens, n * 2 + 3)

            act.wait_ge(s_b2, 1)
            blocks(act, body)

            for m in range(TOP1 // P):
                act.wait_ge(s_m1, m + 1)
                nc.scalar.activation(h1[:, m, :], bank[m][:, :], ACT.Relu, bias=b_top1[:, m:m + 1])\
                    .then_inc(s_h1, 1)
            for m in range(TOP2 // P):
                act.wait_ge(s_m2, m + 1)
                nc.scalar.activation(h2[:, m, :], (bank[4], x1_ps)[m][:, :], ACT.Relu,
                                     bias=b_top2[:, m:m + 1]).then_inc(s_h2, 1)
            act.wait_ge(s_m3, 1)
            nc.scalar.copy(y_sb[:, :], turn_ps[0:1, :]).then_inc(s_ysb, 1)

        @block.vector
        def _(dve):
            dve.sem_inc(s_spread, 1)
            nc.vector.memset(vec_sum[0][0][:, :], 0.0).then_inc(s_vstep, VSTEPS)
            nc.vector.memset(x2[:, :], 0.0).then_inc(s_x2, 2)
            dve.wait_ge(s_early, 16 * EARLY)
            nc.vector.tensor_tensor(w0_pair[:, 0:FULL_CHUNKS, :], w0_pair[:, 0:FULL_CHUNKS, :],
                                    w0_swap[:, 0:FULL_CHUNKS, :], ALU.add).then_inc(s_w0, 1)
            nc.vector.tensor_tensor(w0_pair[0:FIELDS, FULL_CHUNKS, :], w0_pair[0:FIELDS, FULL_CHUNKS, :],
                                    w0_swap[0:FIELDS, FULL_CHUNKS, :], ALU.add).then_inc(s_w0, 1)
            for c in range(SPLITS):
                cs = slice(SPLIT_COLS * c, SPLIT_COLS * (c + 1))
                dve.wait_ge(s_w1h, c + 1)
                nc.vector.tensor_tensor(w1_low[:, cs], w2[:, cs], w1_high[:, cs], ALU.subtract)\
                    .then_inc(s_w1l, 1)
            dve.wait_ge(s_late, 16 * LATE)
            for n in range(2):
                nc.vector.tensor_copy(spread[n][:, FIELDS * TILE_ROWS:G_COLS], row_mask[:, :])\
                    .then_inc(s_mask, 1)

            def products(n, g):
                dve.wait_ge(s_load[g % 2], n * (16 * LOAD_DMAS * GROUPS // 2) + 16 * LOAD_DMAS * (g // 2 + 1))
                p, f = pairs[g % 2], firsts[g % 2]
                nc.vector.tensor_tensor(p[:, 0:FULL_CHUNKS, :], p[:, 0:FULL_CHUNKS, :],
                                        f[:, None, :].to_broadcast([CHUNK_ROWS, FULL_CHUNKS, GROUP]),
                                        ALU.mult)
                nc.vector.tensor_tensor(p[0:LAST_ROWS, FULL_CHUNKS, :], p[0:LAST_ROWS, FULL_CHUNKS, :],
                                        f[0:LAST_ROWS, :], ALU.mult).then_inc(s_prod, 1)

            def take_x1_low(n, g):
                dve.wait_ge(s_x1h, n * GROUPS + (g + 1))
                nc.vector.scalar_tensor_tensor(x1_low[g % 2][:, :], x1_ps[:, :], b0[:, 0:1],
                                               x1_high[g % 2][:, :], ALU.add, ALU.subtract)\
                    .then_inc(s_x1l, 1)

            def halves(n, t):
                u = n * TILES + t
                v = vec_sum[t % 2]
                dve.wait_ge(s_vstep, u * VSTEPS + 2 * VSTEPS)
                nc.vector.tensor_tensor(v[0][:, :], v[0][:, :], v[1][:, :], ALU.add).then_inc(s_comb, 1)
                dve.wait_ge(s_comb, u + 1)
                dve.wait_ge(s_pstep, u * STEPS + 2 * STEPS)
                dve.wait_ge(s_g, u + 1)
                nc.vector.tensor_tensor(x2[:, :], v[0][:, :], pool_out[:, :], ALU.add).then_inc(s_x2, 1)

            def sum_banks(n, t):
                u = n * TILES + t
                v = vec_sum[t % 2]
                step = 0
                for q in range(HALF):
                    k = 2 * q
                    dve.wait_ge(s_y, u * BANKS + (k + 1) + 1)
                    if q == 0:
                        dve.wait_ge(s_x2, u + 1)
                    for r, i in enumerate(fields_of(k)):
                        block_ps = bank[k % RING][:, S * r:S * (r + 1)]
                        x0_i = x0_tokens[:, t, i:i + 1]
                        if step >= 2:
                            dve.wait_ge(s_vstep, u * VSTEPS + (VSTEPS + step - 1))
                        if step == 1:
                            ins = nc.vector.tensor_scalar(v[1][:, :], block_ps, x0_i, None, ALU.mult)
                        else:
                            ins = nc.vector.scalar_tensor_tensor(
                                v[step % 2][:, :], block_ps, x0_i,
                                b1_row[:, :] if step == 0 else v[step % 2][:, :], ALU.mult, ALU.add)
                        ins.then_inc(s_vstep, 1)
                        step += 1
                    if q == 1 and t >= 1:
                        halves(n, t - 1)

            def spread_rows(n, t):
                u = n * TILES + t
                dve.wait_ge(s_g, (u if t == 0 else u - 1) + 1)
                dve.wait_ge(s_mask, 2)
                nc.vector.tensor_tensor(
                    spread[t % 2][:, 0:FIELDS * TILE_ROWS].rearrange("p (i b) -> p i b", b=TILE_ROWS),
                    x0_tokens[:, t, :, None].to_broadcast([P, FIELDS, TILE_ROWS]),
                    row_mask[:, None, :].to_broadcast([P, FIELDS, TILE_ROWS]), ALU.mult)\
                    .then_inc(s_spread, 1)

            products(0, 0)
            take_x1_low(0, 0)

            def body(n, more):
                for t in range(TILES):
                    if t == 0:
                        dve.wait_ge(s_tokens, n * 2 + 1)
                    if t == TILES // 2:
                        dve.wait_ge(s_tokens, n * 2 + 2)
                    sum_banks(n, t)
                    g = t // GROUP_TILES
                    spread_rows(n, t)
                    if t % GROUP_TILES == 1 and g + 1 < GROUPS:
                        products(n, g + 1)
                    if t % GROUP_TILES == 2 and g + 1 < GROUPS:
                        take_x1_low(n, g + 1)
                    if more and t == TILES - 2:
                        products(n + 1, 0)
                halves(n, TILES - 1)
                if more:
                    take_x1_low(n + 1, 0)

            blocks(dve, body)


_OUT = ("y", (ROWS, 1), F32)


def kernel(**inputs):
    import concourse.bacc as _bacc
    from concourse.bass_utils import run_bass_kernel_spmd as _run

    w0 = np.asarray(inputs["L0_rec_w0"]).reshape(FIELDS, FIELDS, S)

    def pair_rows(shift, swapped):
        i = np.arange(FIELDS)
        j = (i + shift) % FIELDS
        return w0[j, i] if swapped else w0[i, j]

    def chunks(swapped):
        return np.stack([np.concatenate([pair_rows(CHUNK_SHIFTS * c + r + 1, swapped)
                                         for r in range(CHUNK_SHIFTS)]) for c in range(FULL_CHUNKS)], axis=1)

    arrays = {f"tbl_{f}": inputs[f"tbl_{f}"] for f in range(FIELDS)}
    arrays["ids"] = np.asarray(inputs["ids"]).reshape(BLOCKS, P, FIELDS).transpose(1, 0, 2).reshape(P, -1)
    arrays["ident"] = np.eye(P, dtype=np.float32)
    arrays["row_mask"] = np.kron(np.eye(TILE_ROWS, dtype=np.float32), np.ones((D, 1), np.float32))
    arrays["w0_pair"], arrays["w0_swap"] = chunks(False), chunks(True)
    arrays["w0_pair_last"] = np.concatenate([pair_rows(SHIFTS - 1, False), pair_rows(0, False)])
    arrays["w0_swap_last"] = pair_rows(SHIFTS - 1, True)
    for w in ("w1", "w2"):
        arrays[w] = np.asarray(inputs[f"L0_rec_{w}"]).reshape(FIELDS, P, S).transpose(1, 0, 2).reshape(P, -1)
    arrays["b0"] = np.asarray(inputs["L0_rec_b0"]).reshape(P, 1)
    arrays["b1"] = np.asarray(inputs["L0_rec_b1"]).reshape(1, S)
    arrays["b2"] = np.asarray(inputs["L0_rec_b2"]).reshape(P, 1)
    top1 = np.asarray(inputs["W_top1"])
    arrays["w_top1"] = top1[0:2 * P].reshape(2, P, TOP1).transpose(1, 0, 2)
    arrays["w_top1c"] = top1[2 * P:]
    arrays["w_top2"] = np.asarray(inputs["W_top2"]).reshape(TOP1 // P, P, TOP2).transpose(1, 0, 2)
    arrays["w_top3"] = np.asarray(inputs["W_top3"]).reshape(TOP2 // P, P).T
    arrays["b_top1"] = np.asarray(inputs["b_top1"]).reshape(TOP1 // P, P).T
    arrays["b_top2"] = np.asarray(inputs["b_top2"]).reshape(TOP2 // P, P).T
    arrays["ctx_t"] = np.asarray(inputs["dense_ctx"]).T
    arrays = {k: np.ascontiguousarray(v) for k, v in arrays.items()}

    nc = _bacc.Bacc("TRN2", target_bir_lowering=False, num_devices=1)
    a = {k: nc.dram_tensor(f"in_{k}", v.shape, mybir.dt.from_np(v.dtype), kind="ExternalInput").ap()
         for k, v in arrays.items()}
    name, shape, dt = _OUT
    out = nc.dram_tensor(name, shape, dt, kind="ExternalOutput").ap()
    dlrm_tower(nc, a, out.rearrange("b a -> a b"))
    r = _run(nc, [{f"in_{k}": v for k, v in arrays.items()}], core_ids=[0])
    return r.results[0][name]
```

```python
from contextlib import ExitStack

import numpy as np

import concourse.bass as bass
import concourse.mybir as mybir

F32 = mybir.dt.float32
F32R = mybir.dt.float32r
I32 = mybir.dt.int32
ALU = mybir.AluOpType
ACT = mybir.ActivationFunctionType

P = 128
FIELDS = 39
D = 16
ROWS = 512
S = 128
GROUP_ROWS = 32
GROUP = GROUP_ROWS * D
GROUPS = 4
BLOCK_ROWS = GROUPS * GROUP_ROWS
BLOCKS = ROWS // BLOCK_ROWS
TILE = P
TILE_ROWS = TILE // D
GROUP_TILES = GROUP // TILE
TILES = GROUPS * GROUP_TILES
GATHER_FIELDS = P // GROUP_ROWS
GATHERS = (FIELDS + GATHER_FIELDS - 1) // GATHER_FIELDS
LAST_GATHER = (FIELDS - (GATHERS - 1) * GATHER_FIELDS) * GROUP_ROWS
SHIFTS = (FIELDS + 1) // 2
CHUNK_SHIFTS = 3
CHUNK_ROWS = CHUNK_SHIFTS * FIELDS
FULL_CHUNKS = (SHIFTS - 2) // CHUNK_SHIFTS
CHUNKS = FULL_CHUNKS + 1
LAST_ROWS = 2 * FIELDS
WRAP_GATHERS = (SHIFTS - 1 + GATHER_FIELDS - 1) // GATHER_FIELDS
SCRATCH_ROWS = FIELDS + WRAP_GATHERS * GATHER_FIELDS
BANK_FIELDS = 4
BANKS = (FIELDS + BANK_FIELDS - 1) // BANK_FIELDS
RING = BANKS // 2
HALF = BANKS // 2
G_COLS = (FIELDS + 1) * TILE_ROWS
TOP1, TOP2 = 512, 256
CTX = 16

GATHERS_OF_TILE = (4, 4, 2, 0)
SPLITS = 4
SPLIT_COLS = FIELDS * S // SPLITS
VSTEPS = HALF * BANK_FIELDS
STEPS = HALF - 1
STORE_DMAS = 3
LOAD_DMAS = 7
PRODUCTS_AT = ((0, 4), (1, 0), (1, 2), (1, 4), (2, 0), (2, 2), (2, 4))
LAYER0_AT = ((1, 1), (1, 4), (1, 7), (2, 1), (2, 4), (2, 7), (3, 1))
X1_HIGH_AT = (3, 1)
X1_LOW_AT = (3, 3)
LAYER0_AT_END = 3


def fields_of(bank):
    return range(BANK_FIELDS * bank, min(BANK_FIELDS * (bank + 1), FIELDS))


def dlrm_tower(nc, a, out):
    ctx = ExitStack()
    with ctx:
        def sb(name, shape, dt=F32):
            return ctx.enter_context(nc.sbuf_tensor(name, shape, dt))

        def pb(name):
            return ctx.enter_context(nc.psum_tensor(name, [P, 512], F32))

        def sem(name):
            return ctx.enter_context(nc.semaphore(name))

        ident = sb("ident", [P, P])
        ids_all = sb("ids_all", [P, BLOCKS * GROUPS * GATHERS], I32)
        field_base = sb("field_base", [P, BLOCKS * GROUPS * GATHERS], I32)
        ids_block = sb("ids_block", [P, GROUPS * GATHERS], I32)
        w0_pair = sb("w0_pair", [CHUNK_ROWS, CHUNKS, S])
        w0_swap = sb("w0_swap", [CHUNK_ROWS, CHUNKS, S])
        w1_high = sb("w1_high", [P, FIELDS * S], F32R)
        w1_low = sb("w1_low", [P, FIELDS * S], F32R)
        w2 = sb("w2", [P, FIELDS * S])
        w_top1 = sb("w_top1", [P, 2, TOP1])
        w_top1c = sb("w_top1c", [CTX, TOP1])
        w_top2 = sb("w_top2", [P, TOP1 // P, TOP2])
        w_top3 = sb("w_top3", [P, TOP2 // P])
        b0 = sb("b0", [P, 1])
        b1_row = sb("b1_row", [P, S])
        b2 = sb("b2", [P, 1])
        b2_sum = sb("b2_sum", [P, 1])
        b_top1 = sb("b_top1", [P, TOP1 // P])
        b_top2 = sb("b_top2", [P, TOP2 // P])
        ctx_t = sb("ctx_t", [CTX, ROWS])
        row_mask = sb("row_mask", [P, TILE_ROWS])
        emb = [sb(f"emb{n}", [P, GATHERS * D]) for n in range(2)]
        scratch = [nc.dram_tensor(f"x0_scratch{n}", (SCRATCH_ROWS, GROUP), F32, kind="Internal").ap()
                   for n in range(2)]
        x0_tokens = [sb(f"x0_tokens{n}", [P, GROUP_TILES, FIELDS]) for n in range(2)]
        pairs = [sb(f"pairs{n}", [CHUNK_ROWS, CHUNKS, GROUP]) for n in range(2)]
        firsts = [sb(f"firsts{n}", [CHUNK_ROWS, GROUP]) for n in range(2)]
        x1_high = [sb(f"x1_high{n}", [P, GROUP], F32R) for n in range(2)]
        x1_low = [sb(f"x1_low{n}", [P, GROUP], F32R) for n in range(2)]
        vec_sum = [sb(f"vec_sum{n}", [P, 2 * S]) for n in range(2)]
        scaled = [sb(f"scaled{n}", [P, BANK_FIELDS * S]) for n in range(HALF)]
        pool_sum = [sb(f"pool_sum{n}", [P, BANK_FIELDS * S]) for n in range(2)]
        x2 = sb("x2", [P, S])
        spread = [sb(f"spread{n}", [P, G_COLS]) for n in range(2)]
        g_block = sb("g_block", [P, FIELDS + 1, BLOCK_ROWS])
        z1 = sb("z1", [P, ROWS])
        z2 = sb("z2", [P, ROWS])
        h1 = sb("h1", [P, TOP1 // P, ROWS])
        h2 = sb("h2", [P, TOP2 // P, ROWS])
        y_sb = sb("y_sb", [1, ROWS])
        warm = sb("warm", [P, 1])

        bank = [pb(f"bank{n}") for n in range(RING)]
        x1_ps = pb("x1_ps")
        turn_ps = pb("turn_ps")
        g_ps = pb("g_ps")
        z2_cols = g_ps[:, G_COLS:G_COLS + BLOCK_ROWS]

        s_ids = sem("ids_loaded")
        s_early = sem("early_weights_loaded")
        s_w1 = sem("w1_loaded")
        s_late = sem("late_weights_loaded")
        s_w2 = sem("w2_loaded")
        s_gather = [sem(f"gathered{n}") for n in range(2)]
        s_store = [sem(f"x0_stored{n}") for n in range(2)]
        s_load = [sem(f"operands_loaded{n}") for n in range(2)]
        s_out = sem("out_stored")
        s_idsb = sem("ids_block_ready")
        s_w0 = sem("w0_summed")
        s_w1h = sem("w1_high_ready")
        s_w1l = sem("w1_low_ready")
        s_b2 = sem("b2_summed")
        s_mask = sem("spread_masks_ready")
        s_ids_sum = sem("ids_with_base")
        s_carry = sem("carries_a_wait_of_sp")
        s_tturned = sem("tokens_in_psum")
        s_tokens = sem("x0_tokens_ready")
        s_prod = sem("products_ready")
        s_l0 = sem("layer0_done")
        s_x1h = sem("x1_high_ready")
        s_x1l = sem("x1_low_ready")
        s_y = sem("bank_filled")
        s_vstep = sem("vector_steps")
        s_abank = sem("scalar_bank_scaled")
        s_pstep = sem("pool_steps")
        s_comb = sem("halves_summed")
        s_x2 = sem("x2_ready")
        s_spread = sem("spread_ready")
        s_g = sem("g_in_psum")
        s_gsb = sem("g_block_written")
        s_z2 = sem("z2_in_psum")
        s_z = sem("z_written")
        s_z1 = sem("z1_written")
        s_m1 = sem("top1_in_psum")
        s_h1 = sem("h1_ready")
        s_m2 = sem("top2_in_psum")
        s_h2 = sem("h2_ready")
        s_m3 = sem("top3_in_psum")
        s_ysb = sem("y_ready")

        EARLY, LATE = 6, 10

        block = ctx.enter_context(nc.Block())

        def group_of(n, g):
            return n + g // GROUPS, g % GROUPS

        def blocks(eng, body):
            with eng.Fori(0, BLOCKS - 1) as n:
                body(n, True)
            body(BLOCKS - 1, False)

        @block.sync
        def _(sp):
            sp.dma_start(ids_all[:, :], a["ids"]).then_inc(s_ids, 16)
            sp.dma_start(field_base[:, :], a["field_base"]).then_inc(s_ids, 16)
            sp.dma_start(ident[:, :], a["ident"]).then_inc(s_early, 16)
            sp.dma_start(w0_pair[:, 0:FULL_CHUNKS, :], a["w0_pair"]).then_inc(s_early, 16)
            sp.dma_start(w0_swap[:, 0:FULL_CHUNKS, :], a["w0_swap"]).then_inc(s_early, 16)
            sp.dma_start(w0_pair[0:LAST_ROWS, FULL_CHUNKS, :], a["w0_pair_last"]).then_inc(s_early, 16)
            sp.dma_start(w0_swap[0:FIELDS, FULL_CHUNKS, :], a["w0_swap_last"]).then_inc(s_early, 16)
            sp.dma_start(b0[:, :], a["b0"]).then_inc(s_early, 16)
            sp.dma_start(w2[:, :], a["w1"]).then_inc(s_w1, 16)
            sp.dma_start(b1_row[:, :], a["b1"].to_broadcast([P, S])).then_inc(s_late, 16)
            sp.dma_start(b2[:, :], a["b2"]).then_inc(s_late, 16)
            sp.dma_start(row_mask[:, :], a["row_mask"]).then_inc(s_late, 16)
            sp.dma_start(w_top1[:, :, :], a["w_top1"]).then_inc(s_late, 16)
            sp.dma_start(w_top1c[:, :], a["w_top1c"]).then_inc(s_late, 16)
            sp.dma_start(w_top2[:, :, :], a["w_top2"]).then_inc(s_late, 16)
            sp.dma_start(w_top3[:, :], a["w_top3"]).then_inc(s_late, 16)
            sp.dma_start(b_top1[:, :], a["b_top1"]).then_inc(s_late, 16)
            sp.dma_start(b_top2[:, :], a["b_top2"]).then_inc(s_late, 16)
            sp.dma_start(ctx_t[:, :], a["ctx_t"]).then_inc(s_late, 16)

            def store_group(g):
                for row, first, count, k in ((0, 0, GATHERS - 1, P), (0, GATHERS - 1, 1, LAST_GATHER),
                                             (FIELDS, 0, WRAP_GATHERS, P)):
                    dst = bass.AP(scratch[g % 2].tensor, (row + first * GATHER_FIELDS) * GROUP,
                                  [[D, k], [GATHER_FIELDS * GROUP, count], [1, D]])
                    src = emb[g % 2][0:k, D * first:D * (first + count)].rearrange("p (j d) -> p j d", d=D)
                    sp.dma_start(dst, src).then_inc(s_store[g % 2], 16)

            def load_group(g):
                for c in range(CHUNK_SHIFTS):
                    rows = slice(FIELDS * c, FIELDS * (c + 1))
                    sp.dma_start(firsts[g % 2][rows, :], scratch[g % 2][0:FIELDS, :])\
                        .then_inc(s_load[g % 2], 16)
                    n = CHUNKS if c == 0 else FULL_CHUNKS
                    src = bass.AP(scratch[g % 2].tensor, (c + 1) * GROUP,
                                  [[GROUP, FIELDS], [CHUNK_SHIFTS * GROUP, n], [1, GROUP]])
                    sp.dma_start(pairs[g % 2][rows, 0:n, :], src).then_inc(s_load[g % 2], 16)
                sp.dma_start(pairs[g % 2][FIELDS:LAST_ROWS, FULL_CHUNKS, :],
                             scratch[g % 2][0:FIELDS, :]).then_inc(s_load[g % 2], 16)

            def bring_group(n, g):
                turn = n * (GROUPS // 2) + (g // 2 + 1)
                sp.wait_ge(s_gather[g % 2], turn * (16 * GATHERS))
                sp.sem_inc(s_carry, 1)
                if not (isinstance(n, int) and n * GROUPS + g == 0):
                    sp.wait_ge(s_l0, n * GROUPS + g)
                store_group(g)
                sp.wait_ge(s_store[g % 2], turn * (16 * STORE_DMAS))
                load_group(g)

            bring_group(0, 0)
            sp.wait_ge(s_w1l, 4)
            sp.dma_start(w2[:, :], a["w2"]).then_inc(s_w2, 16)

            def body(n, more):
                for g in range(1, GROUPS + more):
                    bring_group(*group_of(n, g))

            blocks(sp, body)
            sp.wait_ge(s_ysb, 1)
            sp.dma_start(out, y_sb[:, :]).then_inc(s_out, 16)
            sp.wait_ge(s_out, 16)

        @block.gpsimd
        def _(pool):
            pool.wait_ge(s_ids, 32)
            nc.gpsimd.tensor_tensor(ids_all[:, :], ids_all[:, :], field_base[:, :], ALU.add)\
                .then_inc(s_ids_sum, 1)
            pool.wait_ge(s_ids_sum, 1)

            def take_ids(n, groups):
                nc.gpsimd.tensor_copy(ids_block[:, 0:groups * GATHERS],
                                      ids_all[:, bass.ds((n * GROUPS + 2) * GATHERS, groups * GATHERS)])\
                    .then_inc(s_idsb, 1)

            def gather(g, j, ids):
                k = P if j < GATHERS - 1 else LAST_GATHER
                nc.gpsimd.indirect_dma_start(
                    emb[g % 2][0:k, j * D:(j + 1) * D], None, a["tables"],
                    bass.IndirectOffsetOnAxis(ap=ids[0:k, :], axis=0)).then_inc(s_gather[g % 2], 16)

            for g in range(2):
                for j in range(GATHERS):
                    gather(g, j, ids_all[:, g * GATHERS + j:g * GATHERS + j + 1])
            pool.sem_inc(s_pstep, STEPS)

            def sums(n, t):
                u = n * TILES + t
                done = u * STEPS + STEPS
                pool.wait_ge(s_x2, u + 1)
                for q in range(1, HALF):
                    w = len(fields_of(2 * q + 1)) * S
                    pool.wait_ge(s_abank, u * HALF + (HALF + q + 1))
                    pool.wait_ge(s_pstep, done + (q - 1))
                    so_far = scaled[0] if q == 1 else pool_sum[t % 2]
                    nc.gpsimd.tensor_tensor(pool_sum[t % 2][:, 0:w], so_far[:, 0:w], scaled[q][:, 0:w],
                                            ALU.add).then_inc(s_pstep, 1)

            def body(n, more):
                groups = GROUPS if more else GROUPS - 2
                if not (isinstance(n, int) and n == 0):
                    for buf in range(2):
                        pool.wait_ge(s_gather[buf], (n + 1) * (16 * GATHERS * GROUPS // 2)
                                     - 16 * GATHERS * GROUPS // 2 + 16 * GATHERS)
                take_ids(n, groups)
                for t in range(TILES):
                    g, c = t // GROUP_TILES, t % GROUP_TILES
                    ahead = g + 2
                    if g < groups and c == 0:
                        pool.wait_ge(s_idsb, n + 1)
                        pool.wait_ge(s_store[g % 2], n * (GROUPS // 2 * 16 * STORE_DMAS)
                                     + (g // 2 + 1) * (16 * STORE_DMAS))
                    sums(n, t)
                    if g < groups:
                        first = sum(GATHERS_OF_TILE[0:c])
                        for j in range(first, first + GATHERS_OF_TILE[c]):
                            k = g * GATHERS + j
                            gather(ahead, j, ids_block[:, k:k + 1])

            blocks(pool, body)

        @block.tensor
        def _(pe):
            def turn_tokens(g):
                for c in range(GROUP_TILES):
                    mm = nc.tensor.transpose(turn_ps[:, FIELDS * c:FIELDS * (c + 1)],
                                             firsts[g % 2][0:FIELDS, TILE * c:TILE * (c + 1)],
                                             ident[0:FIELDS, 0:FIELDS])
                mm.then_inc(s_tturned, 1)

            def layer0(n, g, c):
                q = n * GROUPS + g
                if c == 0 and not (isinstance(n, int) and n * GROUPS + g == 0):
                    pe.wait_ge(s_x1h, q)
                    pe.wait_ge(s_x1l, q)
                    pe.wait_ge(s_tokens, q)
                pe.wait_ge(s_prod, q * CHUNKS + (c + 1))
                k = CHUNK_ROWS if c < FULL_CHUNKS else LAST_ROWS
                mm = nc.tensor.matmul(x1_ps[:, :], w0_pair[0:k, c, :], pairs[g % 2][0:k, c, :],
                                      start=(c == 0), stop=(c == CHUNKS - 1))
                if c == 0:
                    turn_tokens(g)
                if c == CHUNKS - 1:
                    mm.then_inc(s_l0, 1)

            def layer1(n, t, behind):
                u = n * TILES + t
                if t % GROUP_TILES == 0:
                    q = n * GROUPS + t // GROUP_TILES
                    pe.wait_ge(s_x1h, q + 1)
                    pe.wait_ge(s_x1l, q + 1)
                g = t // GROUP_TILES
                cols = slice(TILE * (t % GROUP_TILES), TILE * (t % GROUP_TILES + 1))
                high, low = x1_high[g % 2][:, cols], x1_low[g % 2][:, cols]
                for k in range(BANKS):
                    before, back = (k - RING, 0) if k >= RING else (k + RING, 1)
                    if before % 2 == 0:
                        pe.wait_ge(s_vstep, u * VSTEPS + VSTEPS * (1 - back)
                                   + BANK_FIELDS * (before // 2 + 1))
                    else:
                        pe.wait_ge(s_abank, u * HALF + HALF * (1 - back) + (before // 2 + 1))
                    w = len(fields_of(k)) * S
                    ws = slice(BANK_FIELDS * S * k, BANK_FIELDS * S * k + w)
                    ps = bank[k % RING][:, 0:w]
                    nc.tensor.matmul(ps, high, w1_high[:, ws], start=True, stop=False)
                    nc.tensor.matmul(ps, high, w1_low[:, ws], start=False, stop=False)
                    nc.tensor.matmul(ps, low, w1_high[:, ws], start=False, stop=True).then_inc(s_y, 1)
                    behind(k)

            def sum_coordinates(n, t):
                u = n * TILES + t
                pe.wait_ge(s_x2, u + 2 + 1)
                pe.wait_ge(s_spread, u + 1 + 1)
                pe.wait_ge(s_gsb, u + 1)
                nc.tensor.matmul(g_ps[:, 0:G_COLS], x2[:, :], spread[t % 2][:, :],
                                 start=True, stop=True).then_inc(s_g, 1)

            def layer2(n):
                pe.wait_ge(s_gsb, (n + 1) * TILES + 1)
                pe.wait_ge(s_z, n + 1)
                pe.wait_ge(s_w2, 16)
                for i in range(FIELDS):
                    mm = nc.tensor.matmul(z2_cols, w2[:, S * i:S * (i + 1)], g_block[:, i, :],
                                          start=(i == 0), stop=(i == FIELDS - 1))
                mm.then_inc(s_z2, 1)

            for s in (s_y, s_g, s_l0, s_z2):
                pe.sem_inc(s, 1)
            pe.wait_ge(s_early, 16 * EARLY)
            pe.wait_ge(s_w0, 2)
            for c in range(CHUNKS):
                layer0(0, 0, c)
            pe.wait_ge(s_w1h, SPLITS)
            pe.wait_ge(s_w1l, SPLITS)

            def body(n, more):
                for t in range(TILES):
                    g, tile = t // GROUP_TILES, t % GROUP_TILES
                    last = g + 1 == GROUPS
                    chunks = CHUNKS - LAYER0_AT_END if last else CHUNKS

                    def behind(k):
                        for c in range(chunks):
                            if LAYER0_AT[c] == (tile, k) and (more or not last):
                                layer0(*group_of(n, g + 1), c)

                    layer1(n, t, behind)
                    if t >= 1:
                        sum_coordinates(n, t - 1)
                if more:
                    for c in range(CHUNKS - LAYER0_AT_END, CHUNKS):
                        layer0(n + 1, 0, c)
                sum_coordinates(n, TILES - 1)
                layer2(n)

            blocks(pe, body)

            pe.wait_ge(s_late, 16 * LATE)
            pe.wait_ge(s_z1, BLOCKS + 1)
            for m in range(TOP1 // P):
                ms = slice(P * m, P * (m + 1))
                nc.tensor.matmul(bank[m][:, :], w_top1c[:, ms], ctx_t[:, :], start=True, stop=False)
                nc.tensor.matmul(bank[m][:, :], w_top1[:, 0, ms], z1[:, :], start=False, stop=False)
            pe.wait_ge(s_z, BLOCKS + 1)
            for m in range(TOP1 // P):
                ms = slice(P * m, P * (m + 1))
                nc.tensor.matmul(bank[m][:, :], w_top1[:, 1, ms], z2[:, :], start=False,
                                 stop=True).then_inc(s_m1, 1)
            for c in range(TOP1 // P):
                pe.wait_ge(s_h1, c + 1)
                for m in range(TOP2 // P):
                    mm = nc.tensor.matmul((bank[4], x1_ps)[m][:, :], w_top2[:, c, P * m:P * (m + 1)],
                                          h1[:, c, :], start=(c == 0), stop=(c == TOP1 // P - 1))
                    if c == TOP1 // P - 1:
                        mm.then_inc(s_m2, 1)
            for c in range(TOP2 // P):
                pe.wait_ge(s_h2, c + 1)
                mm = nc.tensor.matmul(turn_ps[0:1, :], w_top3[:, c:c + 1], h2[:, c, :],
                                      start=(c == 0), stop=(c == TOP2 // P - 1))
            mm.then_inc(s_m3, 1)

        @block.scalar
        def _(act):
            act.wait_ge(s_w1, 16)
            for c in range(SPLITS):
                cs = slice(SPLIT_COLS * c, SPLIT_COLS * (c + 1))
                nc.scalar.copy(w1_high[:, cs], w2[:, cs]).then_inc(s_w1h, 1)
            act.wait_ge(s_late, 16 * LATE)
            nc.scalar.mul(b2_sum[:, :], b2[:, :], float(D)).then_inc(s_b2, 1)

            def take_tokens(n, g):
                q = n * GROUPS + g
                act.wait_ge(s_tturned, q + 1)
                if not (isinstance(n, int) and n * GROUPS + g == 0):
                    act.wait_ge(s_spread, (q - 1) * GROUP_TILES + 1)
                    act.wait_ge(s_abank, (q - 1) * (GROUP_TILES * HALF) + HALF)
                nc.scalar.copy(x0_tokens[g % 2][:, :, :],
                               turn_ps[:, 0:FIELDS * GROUP_TILES].rearrange("p (t f) -> p t f", f=FIELDS))\
                    .then_inc(s_tokens, 1)

            def take_x1_high(n, g):
                act.wait_ge(s_l0, n * GROUPS + (g + 1) + 1)
                nc.scalar.activation(x1_high[g % 2][:, :], x1_ps[:, :], ACT.Identity, bias=b0[:, 0:1])\
                    .then_inc(s_x1h, 1)

            def scale_banks(n, t, behind):
                u = n * TILES + t
                for q in range(HALF):
                    k = 2 * q + 1
                    act.wait_ge(s_y, u * BANKS + (k + 1) + 1)
                    act.wait_ge(s_pstep, u * STEPS + max(q, 1))
                    for r, i in enumerate(fields_of(k)):
                        ins = nc.scalar.activation(scaled[q][:, S * r:S * (r + 1)],
                                                   bank[k % RING][:, S * r:S * (r + 1)], ACT.Copy,
                                                   scale=x0_tokens[t // GROUP_TILES % 2][:, t % GROUP_TILES, i:i + 1])
                    ins.then_inc(s_abank, 1)
                    behind(q)

            def take_g(n, t):
                u = n * TILES + t
                act.wait_ge(s_g, u + 1 + 1)
                if t == 0:
                    act.wait_ge(s_z2, n + 1)
                    act.wait_ge(s_z1, n + 1)
                nc.scalar.copy(g_block[:, :, TILE_ROWS * t:TILE_ROWS * (t + 1)],
                               g_ps[:, 0:G_COLS].rearrange("p (i b) -> p i b", b=TILE_ROWS))\
                    .then_inc(s_gsb, 1)

            for s in (s_gsb, s_z, s_z1):
                act.sem_inc(s, 1)
            nc.scalar.copy(warm[:, :], b2[:, :]).then_inc(s_abank, HALF)
            take_tokens(0, 0)
            act.wait_ge(s_early, 16 * EARLY)
            take_x1_high(0, 0)

            def body(n, more):
                for t in range(TILES):
                    g, tile = t // GROUP_TILES, t % GROUP_TILES
                    if tile == 0:
                        act.wait_ge(s_tokens, n * GROUPS + (g + 1))

                    def behind(q):
                        if (tile, q) == X1_HIGH_AT and g + 1 < GROUPS:
                            act.wait_ge(s_y, n * (BANKS * TILES) + g * BANKS * GROUP_TILES + 1)
                            take_x1_high(n, g + 1)

                    scale_banks(n, t, behind)
                    if t >= 1:
                        take_g(n, t - 1)
                    if (more or g + 1 < GROUPS) and tile == 1:
                        take_tokens(*group_of(n, g + 1))
                if more:
                    act.wait_ge(s_y, n * (BANKS * TILES) + (GROUPS - 1) * BANKS * GROUP_TILES + 1)
                    take_x1_high(n + 1, 0)
                take_g(n, TILES - 1)
                act.wait_ge(s_gsb, (n + 1) * TILES + 1)
                nc.scalar.copy(z1[:, bass.ds(n * BLOCK_ROWS, BLOCK_ROWS)], g_block[:, FIELDS, :])\
                    .then_inc(s_z1, 1)
                act.wait_ge(s_z2, n + 1 + 1)
                nc.scalar.activation(z2[:, bass.ds(n * BLOCK_ROWS, BLOCK_ROWS)], z2_cols, ACT.Identity,
                                     bias=b2_sum[:, 0:1]).then_inc(s_z, 1)
            act.wait_ge(s_b2, 1)
            blocks(act, body)

            for m in range(TOP1 // P):
                act.wait_ge(s_m1, m + 1)
                nc.scalar.activation(h1[:, m, :], bank[m][:, :], ACT.Relu, bias=b_top1[:, m:m + 1])\
                    .then_inc(s_h1, 1)
            for m in range(TOP2 // P):
                act.wait_ge(s_m2, m + 1)
                nc.scalar.activation(h2[:, m, :], (bank[4], x1_ps)[m][:, :], ACT.Relu,
                                     bias=b_top2[:, m:m + 1]).then_inc(s_h2, 1)
            act.wait_ge(s_m3, 1)
            nc.scalar.copy(y_sb[:, :], turn_ps[0:1, :]).then_inc(s_ysb, 1)

        @block.vector
        def _(dve):
            dve.sem_inc(s_spread, 1)
            nc.vector.memset(vec_sum[0][:, :], 0.0).then_inc(s_vstep, VSTEPS)
            nc.vector.memset(x2[:, :], 0.0).then_inc(s_x2, 2)
            dve.wait_ge(s_early, 16 * EARLY)
            nc.vector.tensor_tensor(w0_pair[:, 0:FULL_CHUNKS, :], w0_pair[:, 0:FULL_CHUNKS, :],
                                    w0_swap[:, 0:FULL_CHUNKS, :], ALU.add).then_inc(s_w0, 1)
            nc.vector.tensor_tensor(w0_pair[0:FIELDS, FULL_CHUNKS, :], w0_pair[0:FIELDS, FULL_CHUNKS, :],
                                    w0_swap[0:FIELDS, FULL_CHUNKS, :], ALU.add).then_inc(s_w0, 1)
            for c in range(SPLITS):
                cs = slice(SPLIT_COLS * c, SPLIT_COLS * (c + 1))
                dve.wait_ge(s_w1h, c + 1)
                nc.vector.tensor_tensor(w1_low[:, cs], w2[:, cs], w1_high[:, cs], ALU.subtract)\
                    .then_inc(s_w1l, 1)
            dve.wait_ge(s_late, 16 * LATE)
            for n in range(2):
                nc.vector.tensor_copy(spread[n][:, FIELDS * TILE_ROWS:G_COLS], row_mask[:, :])\
                    .then_inc(s_mask, 1)

            def products(n, g, c):
                if c == 0:
                    dve.wait_ge(s_load[g % 2], n * (16 * LOAD_DMAS * GROUPS // 2)
                                + 16 * LOAD_DMAS * (g // 2 + 1))
                k = CHUNK_ROWS if c < FULL_CHUNKS else LAST_ROWS
                p = pairs[g % 2][0:k, c, :]
                nc.vector.tensor_tensor(p, p, firsts[g % 2][0:k, :], ALU.mult).then_inc(s_prod, 1)

            def take_x1_low(n, g):
                dve.wait_ge(s_x1h, n * GROUPS + (g + 1))
                nc.vector.scalar_tensor_tensor(x1_low[g % 2][:, :], x1_ps[:, :], b0[:, 0:1],
                                               x1_high[g % 2][:, :], ALU.add, ALU.subtract)\
                    .then_inc(s_x1l, 1)

            def close_sum(n, t):
                u = n * TILES + t
                v = vec_sum[t % 2]
                dve.wait_ge(s_vstep, u * VSTEPS + 2 * VSTEPS)
                dve.wait_ge(s_pstep, u * STEPS + 2 * STEPS)
                for c in range(2):
                    if c == 1:
                        dve.wait_ge(s_comb, u * 2 + 1)
                    nc.vector.tensor_tensor(v[:, :], v[:, :], pool_sum[t % 2][:, 2 * S * c:2 * S * (c + 1)],
                                            ALU.add).then_inc(s_comb, 1)
                dve.wait_ge(s_comb, u * 2 + 2)
                dve.wait_ge(s_g, u + 1)
                nc.vector.tensor_tensor(x2[:, :], v[:, 0:S], v[:, S:2 * S], ALU.add).then_inc(s_x2, 1)

            def sum_banks(n, t, behind):
                u = n * TILES + t
                v = [vec_sum[t % 2][:, S * m:S * (m + 1)] for m in range(2)]
                step = 0
                for q in range(HALF):
                    k = 2 * q
                    dve.wait_ge(s_y, u * BANKS + (k + 1) + 1)
                    if q == 0:
                        dve.wait_ge(s_x2, u + 1)
                    for r, i in enumerate(fields_of(k)):
                        block_ps = bank[k % RING][:, S * r:S * (r + 1)]
                        x0_i = x0_tokens[t // GROUP_TILES % 2][:, t % GROUP_TILES, i:i + 1]
                        if step >= 2:
                            dve.wait_ge(s_vstep, u * VSTEPS + (VSTEPS + step - 1))
                        if step == 1:
                            ins = nc.vector.tensor_scalar(v[1], block_ps, x0_i, None, ALU.mult)
                        else:
                            ins = nc.vector.scalar_tensor_tensor(
                                v[step % 2], block_ps, x0_i,
                                b1_row[:, :] if step == 0 else v[step % 2], ALU.mult, ALU.add)
                        ins.then_inc(s_vstep, 1)
                        step += 1
                    if q == 1 and t >= 1:
                        close_sum(n, t - 1)
                    behind(q)

            def spread_rows(n, t):
                u = n * TILES + t
                dve.wait_ge(s_g, (u if t == 0 else u - 1) + 1)
                dve.wait_ge(s_mask, 2)
                nc.vector.tensor_tensor(
                    spread[t % 2][:, 0:FIELDS * TILE_ROWS].rearrange("p (i b) -> p i b", b=TILE_ROWS),
                    x0_tokens[t // GROUP_TILES % 2][:, t % GROUP_TILES, :, None].to_broadcast([P, FIELDS, TILE_ROWS]),
                    row_mask[:, None, :].to_broadcast([P, FIELDS, TILE_ROWS]), ALU.mult)\
                    .then_inc(s_spread, 1)

            for c in range(CHUNKS):
                products(0, 0, c)
            take_x1_low(0, 0)

            def body(n, more):
                for t in range(TILES):
                    g, tile = t // GROUP_TILES, t % GROUP_TILES
                    ahead = more or g + 1 < GROUPS
                    if tile == 0:
                        dve.wait_ge(s_tokens, n * GROUPS + (g + 1))

                    def behind(q):
                        for c in range(CHUNKS):
                            if ahead and PRODUCTS_AT[c] == (tile, q):
                                products(*group_of(n, g + 1), c)
                        if (tile, q) == X1_LOW_AT and g + 1 < GROUPS:
                            take_x1_low(n, g + 1)

                    sum_banks(n, t, behind)
                    spread_rows(n, t)
                close_sum(n, TILES - 1)
                if more:
                    take_x1_low(n + 1, 0)

            blocks(dve, body)


_OUT = ("y", (ROWS, 1), F32)


def kernel(**inputs):
    import concourse.bacc as _bacc
    from concourse.bass_utils import run_bass_kernel_spmd as _run

    w0 = np.asarray(inputs["L0_rec_w0"]).reshape(FIELDS, FIELDS, S)

    def pair_rows(shift, swapped):
        i = np.arange(FIELDS)
        j = (i + shift) % FIELDS
        return w0[j, i] if swapped else w0[i, j]

    def chunks(swapped):
        return np.stack([np.concatenate([pair_rows(CHUNK_SHIFTS * c + r + 1, swapped)
                                         for r in range(CHUNK_SHIFTS)]) for c in range(FULL_CHUNKS)], axis=1)

    tables = [np.asarray(inputs[f"tbl_{f}"]) for f in range(FIELDS)]
    base = np.cumsum([0] + [len(x) for x in tables])
    arrays = {"tables": np.concatenate(tables)}
    ids = np.zeros((BLOCKS * GROUPS, GROUP_ROWS, GATHERS * GATHER_FIELDS), np.int32)
    ids[:, :, 0:FIELDS] = np.asarray(inputs["ids"]).reshape(-1, GROUP_ROWS, FIELDS)
    first = np.zeros_like(ids)
    first[:, :, 0:FIELDS] = base[0:FIELDS]

    def by_partition(x):
        return x.reshape(-1, GROUP_ROWS, GATHERS, GATHER_FIELDS).transpose(3, 1, 0, 2).reshape(P, -1)

    arrays["ids"], arrays["field_base"] = by_partition(ids), by_partition(first)
    arrays["ident"] = np.eye(P, dtype=np.float32)
    arrays["row_mask"] = np.kron(np.eye(TILE_ROWS, dtype=np.float32), np.ones((D, 1), np.float32))
    arrays["w0_pair"], arrays["w0_swap"] = chunks(False), chunks(True)
    arrays["w0_pair_last"] = np.concatenate([pair_rows(SHIFTS - 1, False), pair_rows(0, False)])
    arrays["w0_swap_last"] = pair_rows(SHIFTS - 1, True)
    for w in ("w1", "w2"):
        arrays[w] = np.asarray(inputs[f"L0_rec_{w}"]).reshape(FIELDS, P, S).transpose(1, 0, 2).reshape(P, -1)
    arrays["b0"] = np.asarray(inputs["L0_rec_b0"]).reshape(P, 1)
    arrays["b1"] = np.asarray(inputs["L0_rec_b1"]).reshape(1, S)
    arrays["b2"] = np.asarray(inputs["L0_rec_b2"]).reshape(P, 1)
    top1 = np.asarray(inputs["W_top1"])
    arrays["w_top1"] = top1[0:2 * P].reshape(2, P, TOP1).transpose(1, 0, 2)
    arrays["w_top1c"] = top1[2 * P:]
    arrays["w_top2"] = np.asarray(inputs["W_top2"]).reshape(TOP1 // P, P, TOP2).transpose(1, 0, 2)
    arrays["w_top3"] = np.asarray(inputs["W_top3"]).reshape(TOP2 // P, P).T
    arrays["b_top1"] = np.asarray(inputs["b_top1"]).reshape(TOP1 // P, P).T
    arrays["b_top2"] = np.asarray(inputs["b_top2"]).reshape(TOP2 // P, P).T
    arrays["ctx_t"] = np.asarray(inputs["dense_ctx"]).T
    arrays = {k: np.ascontiguousarray(v) for k, v in arrays.items()}

    nc = _bacc.Bacc("TRN2", target_bir_lowering=False, num_devices=1)
    a = {k: nc.dram_tensor(f"in_{k}", v.shape, mybir.dt.from_np(v.dtype), kind="ExternalInput").ap()
         for k, v in arrays.items()}
    name, shape, dt = _OUT
    out = nc.dram_tensor(name, shape, dt, kind="ExternalOutput").ap()
    dlrm_tower(nc, a, out.rearrange("b a -> a b"))
    r = _run(nc, [{f"in_{k}": v for k, v in arrays.items()}], core_ids=[0])
    return r.results[0][name]
```

```python
from contextlib import ExitStack

import numpy as np

import concourse.bass as bass
import concourse.mybir as mybir

F32 = mybir.dt.float32
F32R = mybir.dt.float32r
I32 = mybir.dt.int32
ALU = mybir.AluOpType
ACT = mybir.ActivationFunctionType

P = 128
FIELDS = 39
D = 16
ROWS = 512
S = 128
GROUP_ROWS = 32
GROUP = GROUP_ROWS * D
GROUPS = 4
BLOCK_ROWS = GROUPS * GROUP_ROWS
BLOCKS = ROWS // BLOCK_ROWS
TILE = P
TILE_ROWS = TILE // D
GROUP_TILES = GROUP // TILE
TILES = GROUPS * GROUP_TILES
GATHER_FIELDS = P // GROUP_ROWS
GATHERS = (FIELDS + GATHER_FIELDS - 1) // GATHER_FIELDS
LAST_GATHER = (FIELDS - (GATHERS - 1) * GATHER_FIELDS) * GROUP_ROWS
SHIFTS = (FIELDS + 1) // 2
CHUNK_SHIFTS = 3
CHUNK_ROWS = CHUNK_SHIFTS * FIELDS
FULL_CHUNKS = (SHIFTS - 2) // CHUNK_SHIFTS
CHUNKS = FULL_CHUNKS + 1
LAST_ROWS = 2 * FIELDS
WRAP_GATHERS = (SHIFTS - 1 + GATHER_FIELDS - 1) // GATHER_FIELDS
SCRATCH_ROWS = FIELDS + WRAP_GATHERS * GATHER_FIELDS
BANK_FIELDS = 4
BANKS = (FIELDS + BANK_FIELDS - 1) // BANK_FIELDS
SHORT_BANK = 4
SHORT = BANKS * BANK_FIELDS - FIELDS
RING = BANKS // 2
HALF = BANKS // 2
EXTRA_BANK = 4
VEC_BANKS = [k for k in range(0, BANKS, 2) if k != EXTRA_BANK]
ACT_BANKS = sorted([*range(1, BANKS, 2), EXTRA_BANK])
G_COLS = (FIELDS + 1) * TILE_ROWS
TOP1, TOP2 = 512, 256
CTX = 16
TOP_PARTS = ((0, ROWS - BLOCK_ROWS), (ROWS - BLOCK_ROWS, ROWS))

GATHERS_OF_TILE = (3, 2, 3, 2)
EARLIER = GROUP_TILES // 2
SPLITS = 4
SPLIT_COLS = FIELDS * S // SPLITS
STEPS = HALF - 1
COMBS = 3
STORE_DMAS = 3
PART_OF_CHUNK = (0, 0, 1, 1, 2, 2, 2)
LOAD_DMAS = [sum(1 + (c == 0) + (c == FULL_CHUNKS) for c in range(CHUNKS) if PART_OF_CHUNK[c] == part)
             for part in range(3)]


def fields_of(bank):
    first = BANK_FIELDS * bank - (bank > SHORT_BANK) * SHORT
    return range(first, first + BANK_FIELDS - (bank == SHORT_BANK) * SHORT)


VSTEPS = sum(len(fields_of(k)) for k in VEC_BANKS)
EXTRA_COLS = len(fields_of(EXTRA_BANK)) * S
VEC, POOL, NATIVE = range(3)
LOW_BY = (NATIVE, VEC, POOL, NATIVE, VEC, VEC, NATIVE)
SPLIT_CHUNKS = [c for c in range(CHUNKS) if LOW_BY[c] != NATIVE]
SLOTS = 3
PRODUCTS_AT = ((0, 0), (0, 2), (1, 0), (1, 1), (1, 3), (2, 0), (2, 2))
HIGH_AT = ((0, 1), (0, 3), (1, 1), (1, 2), (1, 4), (2, 2), (2, 3))
LOW_AT = ((0, 2), (0, 4), (1, 2), (1, 3), (2, 0), (2, 3), (2, 4))
LAYER0_AT = ((0, 9), (1, 3), (2, 2), (2, 2), (2, 8), (3, 3), (3, 3))
X1_HIGH_AT = (3, 2)
X1_LOW_AT = (3, 3)
WARM_PRODUCTS = 5
SUM_AT = 8
CLOSE_AT = 1
TAKE_G_AT = 4
LAYER2_FROM, LAYER2_FIELDS = 1, 5


def dlrm_tower(nc, a, out):
    ctx = ExitStack()
    with ctx:
        def sb(name, shape, dt=F32):
            return ctx.enter_context(nc.sbuf_tensor(name, shape, dt))

        def pb(name):
            return ctx.enter_context(nc.psum_tensor(name, [P, 512], F32))

        def sem(name):
            return ctx.enter_context(nc.semaphore(name))

        ident = sb("ident", [P, P])
        ids_all = sb("ids_all", [P, BLOCKS * GROUPS * GATHERS], I32)
        field_base = sb("field_base", [P, BLOCKS * GROUPS * GATHERS], I32)
        ids_block = sb("ids_block", [P, (GROUPS + 1) * GATHERS], I32)
        w0_pair = sb("w0_pair", [CHUNK_ROWS, CHUNKS, S])
        w0_swap = sb("w0_swap", [CHUNK_ROWS, CHUNKS, S])
        w0_high = sb("w0_high", [CHUNK_ROWS, CHUNKS, S], F32R)
        w0_low = sb("w0_low", [CHUNK_ROWS, CHUNKS, S], F32R)
        w1_high = sb("w1_high", [P, FIELDS * S], F32R)
        w1_low = sb("w1_low", [P, FIELDS * S], F32R)
        w2 = sb("w2", [P, FIELDS * S])
        w_top1 = sb("w_top1", [P, 2, TOP1])
        w_top1c = sb("w_top1c", [CTX, TOP1])
        w_top2 = sb("w_top2", [P, TOP1 // P, TOP2])
        w_top3 = sb("w_top3", [P, TOP2 // P])
        b0 = sb("b0", [P, 1])
        b1_row = sb("b1_row", [P, S])
        b2 = sb("b2", [P, 1])
        b2_sum = sb("b2_sum", [P, 1])
        b_top1 = sb("b_top1", [P, TOP1 // P])
        b_top2 = sb("b_top2", [P, TOP2 // P])
        ctx_t = sb("ctx_t", [CTX, ROWS])
        row_mask = sb("row_mask", [P, TILE_ROWS])
        emb = [sb(f"emb{n}", [P, GATHERS * D]) for n in range(2)]
        scratch = [nc.dram_tensor(f"x0_scratch{n}", (SCRATCH_ROWS, GROUP), F32, kind="Internal").ap()
                   for n in range(2)]
        x0_tokens = [sb(f"x0_tokens{n}", [P, GROUP_TILES, FIELDS]) for n in range(2)]
        pairs = [sb(f"pairs{n}", [CHUNK_ROWS, CHUNKS, GROUP]) for n in range(2)]
        pair_high = [sb(f"pair_high{n}", [CHUNK_ROWS, GROUP], F32R) for n in range(SLOTS)]
        pair_low = [sb(f"pair_low{n}", [CHUNK_ROWS, GROUP], F32R) for n in range(SLOTS)]
        firsts = [sb(f"firsts{n}", [CHUNK_ROWS, GROUP]) for n in range(2)]
        x1_high = [sb(f"x1_high{n}", [P, GROUP], F32R) for n in range(2)]
        x1_low = [sb(f"x1_low{n}", [P, GROUP], F32R) for n in range(2)]
        vec_sum = [sb(f"vec_sum{n}", [P, 2 * S]) for n in range(2)]
        scaled = [sb(f"scaled{n}", [P, BANK_FIELDS * S]) for n in range(HALF)]
        scaled_extra = [sb(f"scaled_extra{n}", [P, EXTRA_COLS]) for n in range(2)]
        pool_sum = [sb(f"pool_sum{n}", [P, BANK_FIELDS * S]) for n in range(2)]
        x2 = sb("x2", [P, S])
        spread = [sb(f"spread{n}", [P, G_COLS]) for n in range(2)]
        g_block = sb("g_block", [P, FIELDS + 1, BLOCK_ROWS])
        z1 = sb("z1", [P, ROWS])
        z2 = sb("z2", [P, ROWS])
        h1 = sb("h1", [P, TOP1 // P, ROWS])
        h2 = sb("h2", [P, TOP2 // P, ROWS])
        y_sb = sb("y_sb", [1, ROWS])
        warm = sb("warm", [P, 1])

        bank = [pb(f"bank{n}") for n in range(RING)]
        x1_ps = pb("x1_ps")
        turn_ps = pb("turn_ps")
        g_ps = pb("g_ps")
        z2_cols = g_ps[:, G_COLS:G_COLS + BLOCK_ROWS]

        s_ids = sem("ids_loaded")
        s_early = sem("early_weights_loaded")
        s_w1 = [sem(f"w1_loaded{c}") for c in range(SPLITS)]
        s_late = sem("late_weights_loaded")
        s_w2 = sem("w2_loaded")
        s_gather = [sem(f"gathered{n}") for n in range(2)]
        s_store = [sem(f"x0_stored{n}") for n in range(2)]
        s_load = [[sem(f"operands{part}_loaded{n}") for n in range(2)] for part in range(3)]
        s_out = sem("out_stored")
        s_idsb = sem("ids_block_ready")
        s_w0 = sem("w0_summed")
        s_w1h = sem("w1_high_ready")
        s_w1l = sem("w1_low_ready")
        s_b2 = sem("b2_summed")
        s_mask = sem("spread_masks_ready")
        s_ids_sum = sem("ids_with_base")
        s_carry = sem("carries_a_wait_of_sp")
        s_tturned = sem("tokens_in_psum")
        s_tokens = sem("x0_tokens_ready")
        s_prod = sem("products_ready")
        s_w0h = sem("w0_high_ready")
        s_w0l = sem("w0_low_ready")
        s_high = sem("pair_high_ready")
        s_low = [sem(f"pair_low_ready_{who}") for who in ("vector", "pool")]
        s_chunk = sem("layer0_chunks_done")
        s_x1h = sem("x1_high_ready")
        s_x1l = sem("x1_low_ready")
        s_y = sem("bank_filled")
        s_vstep = sem("vector_steps")
        s_abank = sem("scalar_bank_scaled")
        s_pstep = sem("pool_steps")
        s_comb = sem("halves_summed")
        s_x2 = sem("x2_ready")
        s_spread = sem("spread_ready")
        s_g = sem("g_in_psum")
        s_gsb = sem("g_block_written")
        s_z2 = sem("z2_in_psum")
        s_z = sem("z_written")
        s_z1 = sem("z1_written")
        s_m1 = sem("top1_in_psum")
        s_h1 = sem("h1_ready")
        s_m2 = sem("top2_in_psum")
        s_h2 = sem("h2_ready")
        s_m3 = sem("top3_in_psum")
        s_ysb = sem("y_ready")

        EARLY, LATE = 9, 7

        block = ctx.enter_context(nc.Block())

        def group_of(n, g):
            return n + g // GROUPS, g % GROUPS

        def rows_of(c):
            return CHUNK_ROWS if c < FULL_CHUNKS else LAST_ROWS

        def take_pair_low(eng, n, g, c):
            q = n * GROUPS + g
            eng.wait_ge(s_high, q * len(SPLIT_CHUNKS) + (SPLIT_CHUNKS.index(c) + 1))
            k, slot = rows_of(c), c % SLOTS
            (nc.vector, nc.gpsimd)[LOW_BY[c]].tensor_tensor(
                pair_low[slot][0:k, :], pairs[g % 2][0:k, c, :], pair_high[slot][0:k, :],
                ALU.subtract).then_inc(s_low[LOW_BY[c]], 1)

        def blocks(eng, body):
            with eng.Fori(0, BLOCKS - 1) as n:
                body(n, True)
            body(BLOCKS - 1, False)

        @block.sync
        def _(sp):
            sp.dma_start(ids_all[:, :], a["ids"]).then_inc(s_ids, 16)
            sp.dma_start(field_base[:, :], a["field_base"]).then_inc(s_ids, 16)
            sp.dma_start(ident[:, :], a["ident"]).then_inc(s_early, 16)
            sp.dma_start(w0_pair[:, 0:FULL_CHUNKS, :], a["w0_pair"]).then_inc(s_early, 16)
            sp.dma_start(w0_swap[:, 0:FULL_CHUNKS, :], a["w0_swap"]).then_inc(s_early, 16)
            sp.dma_start(w0_pair[0:LAST_ROWS, FULL_CHUNKS, :], a["w0_pair_last"]).then_inc(s_early, 16)
            sp.dma_start(w0_swap[0:FIELDS, FULL_CHUNKS, :], a["w0_swap_last"]).then_inc(s_early, 16)
            sp.dma_start(b0[:, :], a["b0"]).then_inc(s_early, 16)
            sp.dma_start(b2[:, :], a["b2"]).then_inc(s_early, 16)
            sp.dma_start(row_mask[:, :], a["row_mask"]).then_inc(s_early, 16)
            sp.dma_start(b1_row[:, :], a["b1"].to_broadcast([P, S])).then_inc(s_early, 16)

            for c in range(SPLITS):
                cs = slice(SPLIT_COLS * c, SPLIT_COLS * (c + 1))
                sp.dma_start(w2[:, cs], a["w1"][:, cs]).then_inc(s_w1[c], 16)

            def store_group(g):
                for row, first, count, k in ((0, 0, GATHERS - 1, P), (0, GATHERS - 1, 1, LAST_GATHER),
                                             (FIELDS, 0, WRAP_GATHERS, P)):
                    dst = bass.AP(scratch[g % 2].tensor, (row + first * GATHER_FIELDS) * GROUP,
                                  [[D, k], [GATHER_FIELDS * GROUP, count], [1, D]])
                    src = emb[g % 2][0:k, D * first:D * (first + count)].rearrange("p (j d) -> p j d", d=D)
                    sp.dma_start(dst, src).then_inc(s_store[g % 2], 16)

            def load_group(g):
                x0 = scratch[g % 2]

                def rotated(shift, count):
                    return bass.AP(x0.tensor, shift * GROUP, [[GROUP, count], [GROUP, FIELDS], [1, GROUP]])

                sp.dma_start(firsts[g % 2][:, :],
                             bass.AP(x0.tensor, 0, [[0, CHUNK_SHIFTS], [GROUP, FIELDS], [1, GROUP]]))\
                    .then_inc(s_load[0][g % 2], 16)
                for c in range(FULL_CHUNKS):
                    sp.dma_start(pairs[g % 2][:, c, :], rotated(CHUNK_SHIFTS * c + 1, CHUNK_SHIFTS))\
                        .then_inc(s_load[PART_OF_CHUNK[c]][g % 2], 16)
                for r, shift in enumerate((SHIFTS - 1, 0)):
                    sp.dma_start(pairs[g % 2][FIELDS * r:FIELDS * (r + 1), FULL_CHUNKS, :],
                                 x0[shift:shift + FIELDS, :]).then_inc(s_load[PART_OF_CHUNK[FULL_CHUNKS]][g % 2], 16)

            def bring_group(n, g):
                turn = n * (GROUPS // 2) + (g // 2 + 1)
                sp.wait_ge(s_gather[g % 2], turn * (16 * GATHERS))
                sp.sem_inc(s_carry, 1)
                if not (isinstance(n, int) and n * GROUPS + g < 2):
                    sp.wait_ge(s_chunk, (n * GROUPS + (g - 1)) * CHUNKS)
                store_group(g)
                sp.wait_ge(s_store[g % 2], turn * (16 * STORE_DMAS))
                load_group(g)

            bring_group(0, 0)
            bring_group(0, 1)
            sp.wait_ge(s_w1l, SPLITS)
            sp.dma_start(w2[:, :], a["w2"]).then_inc(s_w2, 16)
            sp.dma_start(w_top1[:, :, :], a["w_top1"]).then_inc(s_late, 16)
            sp.dma_start(w_top1c[:, :], a["w_top1c"]).then_inc(s_late, 16)
            sp.dma_start(w_top2[:, :, :], a["w_top2"]).then_inc(s_late, 16)
            sp.dma_start(w_top3[:, :], a["w_top3"]).then_inc(s_late, 16)
            sp.dma_start(b_top1[:, :], a["b_top1"]).then_inc(s_late, 16)
            sp.dma_start(b_top2[:, :], a["b_top2"]).then_inc(s_late, 16)
            sp.dma_start(ctx_t[:, :], a["ctx_t"]).then_inc(s_late, 16)

            def body(n, more):
                for g in range(2, GROUPS + 2 * more):
                    bring_group(*group_of(n, g))

            blocks(sp, body)
            sp.wait_ge(s_ysb, len(TOP_PARTS))
            sp.dma_start(out, y_sb[:, :]).then_inc(s_out, 16)
            sp.wait_ge(s_out, 16)

        @block.gpsimd
        def _(pool):
            pool.wait_ge(s_ids, 32)
            nc.gpsimd.tensor_tensor(ids_all[:, :], ids_all[:, :], field_base[:, :], ALU.add)\
                .then_inc(s_ids_sum, 1)
            pool.wait_ge(s_ids_sum, 1)

            def take_ids(n, groups):
                nc.gpsimd.tensor_copy(ids_block[:, 0:groups * GATHERS],
                                      ids_all[:, bass.ds((n * GROUPS + 2) * GATHERS, groups * GATHERS)])\
                    .then_inc(s_idsb, 1)

            def gather(g, j, ids):
                k = P if j < GATHERS - 1 else LAST_GATHER
                nc.gpsimd.indirect_dma_start(
                    emb[g % 2][0:k, j * D:(j + 1) * D], None, a["tables"],
                    bass.IndirectOffsetOnAxis(ap=ids[0:k, :], axis=0)).then_inc(s_gather[g % 2], 16)

            def gathers_before(c):
                return sum(GATHERS_OF_TILE[0:c])

            for g in range(2):
                for j in range(GATHERS):
                    gather(g, j, ids_all[:, g * GATHERS + j:g * GATHERS + j + 1])
            pool.wait_ge(s_store[0], 16 * STORE_DMAS)
            for j in range(gathers_before(EARLIER)):
                gather(2, j, ids_all[:, 2 * GATHERS + j:2 * GATHERS + j + 1])
            pool.sem_inc(s_pstep, STEPS)
            pool.sem_inc(s_low[POOL], LOW_BY.count(POOL))

            def sums(n, t, behind):
                u = n * TILES + t
                done = u * STEPS + STEPS
                behind(0)
                pool.wait_ge(s_x2, u + 1)
                for q in range(1, HALF):
                    pool.wait_ge(s_abank, u * len(ACT_BANKS) + (len(ACT_BANKS) + ACT_BANKS.index(2 * q + 1) + 1))
                    pool.wait_ge(s_pstep, done + (q - 1))
                    so_far = scaled[0] if q == 1 else pool_sum[t % 2]
                    nc.gpsimd.tensor_tensor(pool_sum[t % 2][:, :], so_far[:, :], scaled[q][:, :],
                                            ALU.add).then_inc(s_pstep, 1)
                    behind(q)

            def body(n, more):
                groups = GROUPS + 1 if more else GROUPS - 2
                if not (isinstance(n, int) and n == 0):
                    for buf in range(2):
                        early = gathers_before(EARLIER) if buf == 0 else 0
                        pool.wait_ge(s_gather[buf], n * (16 * GATHERS * GROUPS // 2)
                                     + 16 * GATHERS + 16 * early)
                take_ids(n, groups)
                for t in range(TILES):
                    g, tile = t // GROUP_TILES, t % GROUP_TILES
                    g_then, c = (t + EARLIER) // GROUP_TILES, (t + EARLIER) % GROUP_TILES
                    if t == 0:
                        pool.wait_ge(s_idsb, n + 1)
                    if g_then < groups and c == 0:
                        pool.wait_ge(s_store[g_then % 2], n * (GROUPS // 2 * 16 * STORE_DMAS)
                                     + (g_then // 2 + 1) * (16 * STORE_DMAS))

                    def behind(q):
                        for i in range(CHUNKS):
                            if LOW_BY[i] == POOL and LOW_AT[i] == (tile, q) and (more or g + 1 < GROUPS):
                                take_pair_low(pool, *group_of(n, g + 1), i)
                        if g_then < groups and 1 <= q <= GATHERS_OF_TILE[c]:
                            j = gathers_before(c) + q - 1
                            k = g_then * GATHERS + j
                            gather(g_then + 2, j, ids_block[:, k:k + 1])

                    sums(n, t, behind)

            blocks(pool, body)

        @block.tensor
        def _(pe):
            def turn_tokens(g):
                for c in range(GROUP_TILES):
                    mm = nc.tensor.transpose(turn_ps[:, FIELDS * c:FIELDS * (c + 1)],
                                             firsts[g % 2][0:FIELDS, TILE * c:TILE * (c + 1)],
                                             ident[0:FIELDS, 0:FIELDS])
                mm.then_inc(s_tturned, 1)

            def layer0(n, g, c):
                q = n * GROUPS + g
                if c == 0 and not (isinstance(n, int) and n * GROUPS + g == 0):
                    pe.wait_ge(s_x1h, q)
                    pe.wait_ge(s_x1l, q)
                    pe.wait_ge(s_tokens, q)
                k, first, last = rows_of(c), c == 0, c == CHUNKS - 1
                if LOW_BY[c] == NATIVE or isinstance(n, int) and n * GROUPS + g == 0:
                    pe.wait_ge(s_prod, q * CHUNKS + (c + 1))
                    mm = nc.tensor.matmul(x1_ps[:, :], w0_pair[0:k, c, :], pairs[g % 2][0:k, c, :],
                                          start=first, stop=last)
                else:
                    who = LOW_BY[c]
                    pe.wait_ge(s_low[who], q * LOW_BY.count(who) + LOW_BY[0:c + 1].count(who))
                    high, low = (x[c % SLOTS][0:k, :] for x in (pair_high, pair_low))
                    nc.tensor.matmul(x1_ps[:, :], w0_high[0:k, c, :], high, start=first, stop=False)
                    nc.tensor.matmul(x1_ps[:, :], w0_low[0:k, c, :], high, start=False, stop=False)
                    mm = nc.tensor.matmul(x1_ps[:, :], w0_high[0:k, c, :], low, start=False, stop=last)
                mm.then_inc(s_chunk, 1)
                if c == 0:
                    turn_tokens(g)

            def layer1(n, t, behind):
                u = n * TILES + t
                if t % GROUP_TILES == 0:
                    q = n * GROUPS + t // GROUP_TILES
                    pe.wait_ge(s_x1h, q + 1)
                    pe.wait_ge(s_x1l, q + 1)
                g = t // GROUP_TILES
                cols = slice(TILE * (t % GROUP_TILES), TILE * (t % GROUP_TILES + 1))
                high, low = x1_high[g % 2][:, cols], x1_low[g % 2][:, cols]
                for k in range(BANKS):
                    before, back = (k - RING, 0) if k >= RING else (k + RING, 1)
                    if before in VEC_BANKS:
                        pe.wait_ge(s_vstep, u * VSTEPS + VSTEPS * (1 - back)
                                   + sum(len(fields_of(b)) for b in VEC_BANKS if b <= before))
                    else:
                        pe.wait_ge(s_abank, u * len(ACT_BANKS) + len(ACT_BANKS) * (1 - back)
                                   + (ACT_BANKS.index(before) + 1))
                    w = len(fields_of(k)) * S
                    ws = slice(S * fields_of(k)[0], S * fields_of(k)[0] + w)
                    ps = bank[k % RING][:, 0:w]
                    nc.tensor.matmul(ps, high, w1_high[:, ws], start=True, stop=False)
                    nc.tensor.matmul(ps, high, w1_low[:, ws], start=False, stop=False)
                    nc.tensor.matmul(ps, low, w1_high[:, ws], start=False, stop=True).then_inc(s_y, 1)
                    behind(k)

            def sum_coordinates(n, t):
                u = n * TILES + t
                pe.wait_ge(s_x2, u + 2 + 1)
                pe.wait_ge(s_spread, u + 1 + 1)
                pe.wait_ge(s_gsb, u + 1)
                nc.tensor.matmul(g_ps[:, 0:G_COLS], x2[:, :], spread[t % 2][:, :],
                                 start=True, stop=True).then_inc(s_g, 1)

            def layer2(n, fields):
                if fields[0] == 0:
                    pe.wait_ge(s_gsb, (n + 1) * TILES + 1)
                    pe.wait_ge(s_z, n + 1)
                    pe.wait_ge(s_w2, 16)
                for i in fields:
                    mm = nc.tensor.matmul(z2_cols, w2[:, S * i:S * (i + 1)], g_block[:, i, :],
                                          start=(i == 0), stop=(i == FIELDS - 1))
                if fields[-1] == FIELDS - 1:
                    mm.then_inc(s_z2, 1)

            def top_first(part):
                cols = slice(*TOP_PARTS[part])
                blocks_done = cols.stop // BLOCK_ROWS
                pe.wait_ge(s_late, 16 * LATE)
                if part == 0:
                    pe.wait_ge(s_vstep, (BLOCKS * TILES + 1) * VSTEPS)
                    pe.wait_ge(s_abank, (BLOCKS * TILES + 1) * len(ACT_BANKS))
                else:
                    pe.wait_ge(s_h1, TOP1 // P)
                pe.wait_ge(s_z1, blocks_done + 1)
                for m in range(TOP1 // P):
                    ms = slice(P * m, P * (m + 1))
                    nc.tensor.matmul(bank[m][:, cols], w_top1c[:, ms], ctx_t[:, cols], start=True, stop=False)
                    nc.tensor.matmul(bank[m][:, cols], w_top1[:, 0, ms], z1[:, cols], start=False, stop=False)
                pe.wait_ge(s_z, blocks_done + 1)
                for m in range(TOP1 // P):
                    ms = slice(P * m, P * (m + 1))
                    nc.tensor.matmul(bank[m][:, cols], w_top1[:, 1, ms], z2[:, cols], start=False,
                                     stop=True).then_inc(s_m1, 1)

            def top_rest(part):
                cols = slice(*TOP_PARTS[part])
                if part > 0:
                    pe.wait_ge(s_h2, part * (TOP2 // P))
                    pe.wait_ge(s_ysb, part)
                for c in range(TOP1 // P):
                    pe.wait_ge(s_h1, part * (TOP1 // P) + c + 1)
                    for m in range(TOP2 // P):
                        mm = nc.tensor.matmul((bank[4], x1_ps)[m][:, cols], w_top2[:, c, P * m:P * (m + 1)],
                                              h1[:, c, cols], start=(c == 0), stop=(c == TOP1 // P - 1))
                        if c == TOP1 // P - 1:
                            mm.then_inc(s_m2, 1)
                for c in range(TOP2 // P):
                    pe.wait_ge(s_h2, part * (TOP2 // P) + c + 1)
                    mm = nc.tensor.matmul(turn_ps[0:1, cols], w_top3[:, c:c + 1], h2[:, c, cols],
                                          start=(c == 0), stop=(c == TOP2 // P - 1))
                mm.then_inc(s_m3, 1)

            for s in (s_y, s_g, s_z2):
                pe.sem_inc(s, 1)
            pe.wait_ge(s_early, 16 * EARLY)
            pe.wait_ge(s_w0, 2)
            pe.wait_ge(s_store[0], 16 * STORE_DMAS)
            for c in range(WARM_PRODUCTS):
                nc.tensor.matmul(g_ps[:, :], w0_pair[:, 0, :], w0_pair[:, 0:512 // S, :], start=True, stop=True)
            for c in range(CHUNKS):
                layer0(0, 0, c)
            pe.wait_ge(s_w0h, 2)
            pe.wait_ge(s_w0l, 2)
            pe.wait_ge(s_w1h, SPLITS)
            pe.wait_ge(s_w1l, SPLITS)

            def tile_work(n, t, ahead):
                g, tile = t // GROUP_TILES, t % GROUP_TILES

                def behind(k):
                    for c in range(CHUNKS):
                        if ahead and LAYER0_AT[c] == (tile, k):
                            layer0(*group_of(n, g + 1), c)
                    first = (k - LAYER2_FROM) * LAYER2_FIELDS
                    if t == TILES + 1 and 0 <= first < FIELDS:
                        layer2(n, range(first, min(first + LAYER2_FIELDS, FIELDS)))
                    if k == SUM_AT and t >= 1:
                        sum_coordinates(n, t - 1)

                layer1(n, t, behind)

            def body(n, more):
                for t in range(2, TILES + 2 * more):
                    tile_work(n, t, more or t // GROUP_TILES + 1 < GROUPS)
                if not more:
                    top_first(0)
                    sum_coordinates(n, TILES - 1)
                    top_rest(0)
                    layer2(n, range(FIELDS))

            for t in range(2):
                tile_work(0, t, True)
            blocks(pe, body)

            top_first(1)
            top_rest(1)

        @block.scalar
        def _(act):
            act.wait_ge(s_early, 16 * EARLY)
            nc.scalar.mul(b2_sum[:, :], b2[:, :], float(D)).then_inc(s_b2, 1)

            act.wait_ge(s_w0, 2)
            nc.scalar.copy(w0_high[:, 0:FULL_CHUNKS, :], w0_pair[:, 0:FULL_CHUNKS, :]).then_inc(s_w0h, 1)
            nc.scalar.copy(w0_high[0:LAST_ROWS, FULL_CHUNKS, :], w0_pair[0:LAST_ROWS, FULL_CHUNKS, :])\
                .then_inc(s_w0h, 1)

            def split_w1(c):
                act.wait_ge(s_w1[c], 16)
                cs = slice(SPLIT_COLS * c, SPLIT_COLS * (c + 1))
                nc.scalar.copy(w1_high[:, cs], w2[:, cs]).then_inc(s_w1h, 1)

            def take_tokens(n, g):
                q = n * GROUPS + g
                act.wait_ge(s_tturned, q + 1)
                if not (isinstance(n, int) and n * GROUPS + g == 0):
                    act.wait_ge(s_spread, (q - 1) * GROUP_TILES + 1)
                    act.wait_ge(s_abank, (q - 1) * (GROUP_TILES * len(ACT_BANKS)) + len(ACT_BANKS))
                nc.scalar.copy(x0_tokens[g % 2][:, :, :],
                               turn_ps[:, 0:FIELDS * GROUP_TILES].rearrange("p (t f) -> p t f", f=FIELDS))\
                    .then_inc(s_tokens, 1)

            def take_pair_high(n, g, c):
                q = n * GROUPS + g
                k, slot = rows_of(c), c % SLOTS
                act.wait_ge(s_prod, q * CHUNKS + (c + 1))
                act.wait_ge(s_chunk, q * CHUNKS + max(c + 1 - SLOTS, 0))
                nc.scalar.copy(pair_high[slot][0:k, :], pairs[g % 2][0:k, c, :]).then_inc(s_high, 1)

            def take_x1_high(n, g):
                act.wait_ge(s_chunk, (n * GROUPS + (g + 1)) * CHUNKS)
                nc.scalar.activation(x1_high[g % 2][:, :], x1_ps[:, :], ACT.Identity, bias=b0[:, 0:1])\
                    .then_inc(s_x1h, 1)

            def scale_banks(n, t, behind):
                u = n * TILES + t
                for k in ACT_BANKS:
                    q = k // 2
                    act.wait_ge(s_y, u * BANKS + (k + 1) + 1)
                    if k != EXTRA_BANK:
                        act.wait_ge(s_pstep, u * STEPS + max(q, 1))
                    elif t > 1:
                        act.wait_ge(s_comb, (u - 2) * COMBS + 1)
                    place = scaled_extra[t % 2] if k == EXTRA_BANK else scaled[q]
                    for r, i in enumerate(fields_of(k)):
                        ins = nc.scalar.activation(place[:, S * r:S * (r + 1)],
                                                   bank[k % RING][:, S * r:S * (r + 1)], ACT.Copy,
                                                   scale=x0_tokens[t // GROUP_TILES % 2][:, t % GROUP_TILES, i:i + 1])
                    ins.then_inc(s_abank, 1)
                    if k != EXTRA_BANK:
                        behind(q)

            def take_g(n, t):
                u = n * TILES + t
                act.wait_ge(s_g, u + 1 + 1)
                if t % TILES == 0:
                    act.wait_ge(s_z2, n + (t // TILES + 1))
                    act.wait_ge(s_z1, n + (t // TILES + 1))
                at = TILE_ROWS * (t % TILES)
                nc.scalar.copy(g_block[:, :, at:at + TILE_ROWS],
                               g_ps[:, 0:G_COLS].rearrange("p (i b) -> p i b", b=TILE_ROWS))\
                    .then_inc(s_gsb, 1)

            def top_first(part):
                cols = slice(*TOP_PARTS[part])
                act.wait_ge(s_late, 16 * LATE)
                for m in range(TOP1 // P):
                    act.wait_ge(s_m1, part * (TOP1 // P) + m + 1)
                    nc.scalar.activation(h1[:, m, cols], bank[m][:, cols], ACT.Relu,
                                         bias=b_top1[:, m:m + 1]).then_inc(s_h1, 1)

            def top_rest(part):
                cols = slice(*TOP_PARTS[part])
                for m in range(TOP2 // P):
                    act.wait_ge(s_m2, part * (TOP2 // P) + m + 1)
                    nc.scalar.activation(h2[:, m, cols], (bank[4], x1_ps)[m][:, cols], ACT.Relu,
                                         bias=b_top2[:, m:m + 1]).then_inc(s_h2, 1)
                act.wait_ge(s_m3, part + 1)
                nc.scalar.copy(y_sb[:, cols], turn_ps[0:1, cols]).then_inc(s_ysb, 1)

            for s in (s_gsb, s_z, s_z1):
                act.sem_inc(s, 1)
            act.sem_inc(s_high, len(SPLIT_CHUNKS))
            nc.scalar.copy(warm[:, :], b2[:, :]).then_inc(s_abank, len(ACT_BANKS))
            for c in range(SPLITS):
                split_w1(c)
            take_tokens(0, 0)
            take_x1_high(0, 0)

            def take_z1(n):
                act.wait_ge(s_gsb, (n + 1) * TILES + 1)
                nc.scalar.copy(z1[:, bass.ds(n * BLOCK_ROWS, BLOCK_ROWS)], g_block[:, FIELDS, :])\
                    .then_inc(s_z1, 1)

            def take_z2(n):
                act.wait_ge(s_z2, n + 1 + 1)
                nc.scalar.activation(z2[:, bass.ds(n * BLOCK_ROWS, BLOCK_ROWS)], z2_cols, ACT.Identity,
                                     bias=b2_sum[:, 0:1]).then_inc(s_z, 1)

            def tile_work(n, t, ahead):
                g, tile = t // GROUP_TILES, t % GROUP_TILES
                if tile == 0:
                    act.wait_ge(s_tokens, n * GROUPS + (g + 1))

                def behind(q):
                    for c in SPLIT_CHUNKS:
                        if ahead and HIGH_AT[c] == (tile, q):
                            take_pair_high(*group_of(n, g + 1), c)
                    if (tile, q) == X1_HIGH_AT and ahead:
                        act.wait_ge(s_y, n * (BANKS * TILES) + g * BANKS * GROUP_TILES + 1)
                        take_x1_high(*group_of(n, g + 1))
                    if t == TILES + 1 and q == 0:
                        take_z1(n)
                    if t == TILES + 1 and q == TAKE_G_AT:
                        take_z2(n)
                    if q == TAKE_G_AT and t >= 1:
                        take_g(n, t - 1)

                scale_banks(n, t, behind)
                if ahead and tile == 1:
                    take_tokens(*group_of(n, g + 1))

            def body(n, more):
                for t in range(2, TILES + 2 * more):
                    tile_work(n, t, more or t // GROUP_TILES + 1 < GROUPS)
                if not more:
                    top_first(0)
                    take_g(n, TILES - 1)
                    top_rest(0)
                    take_z1(n)
                    take_z2(n)

            for t in range(2):
                tile_work(0, t, True)
            act.wait_ge(s_b2, 1)
            blocks(act, body)

            top_first(1)
            top_rest(1)

        @block.vector
        def _(dve):
            dve.sem_inc(s_spread, 1)
            nc.vector.memset(vec_sum[0][:, :], 0.0).then_inc(s_vstep, VSTEPS)
            nc.vector.memset(x2[:, :], 0.0).then_inc(s_x2, 2)
            dve.wait_ge(s_early, 16 * EARLY)
            nc.vector.tensor_tensor(w0_pair[:, 0:FULL_CHUNKS, :], w0_pair[:, 0:FULL_CHUNKS, :],
                                    w0_swap[:, 0:FULL_CHUNKS, :], ALU.add).then_inc(s_w0, 1)
            nc.vector.tensor_tensor(w0_pair[0:FIELDS, FULL_CHUNKS, :], w0_pair[0:FIELDS, FULL_CHUNKS, :],
                                    w0_swap[0:FIELDS, FULL_CHUNKS, :], ALU.add).then_inc(s_w0, 1)
            for n in range(2):
                nc.vector.tensor_copy(spread[n][:, FIELDS * TILE_ROWS:G_COLS], row_mask[:, :])\
                    .then_inc(s_mask, 1)

            dve.wait_ge(s_w0h, 2)
            for k, cs in ((CHUNK_ROWS, slice(0, FULL_CHUNKS)), (LAST_ROWS, slice(FULL_CHUNKS, CHUNKS))):
                nc.vector.tensor_tensor(w0_low[0:k, cs, :], w0_pair[0:k, cs, :], w0_high[0:k, cs, :],
                                        ALU.subtract).then_inc(s_w0l, 1)
            dve.sem_inc(s_low[VEC], LOW_BY.count(VEC))

            def split_w1(c):
                cs = slice(SPLIT_COLS * c, SPLIT_COLS * (c + 1))
                dve.wait_ge(s_w1h, c + 1)
                nc.vector.tensor_tensor(w1_low[:, cs], w2[:, cs], w1_high[:, cs], ALU.subtract)\
                    .then_inc(s_w1l, 1)

            def products(n, g, c):
                part = PART_OF_CHUNK[c]
                if c == 0 or part > PART_OF_CHUNK[c - 1]:
                    dve.wait_ge(s_load[part][g % 2], n * (16 * LOAD_DMAS[part] * GROUPS // 2)
                                + 16 * LOAD_DMAS[part] * (g // 2 + 1))
                k = rows_of(c)
                p = pairs[g % 2][0:k, c, :]
                nc.vector.tensor_tensor(p, p, firsts[g % 2][0:k, :], ALU.mult).then_inc(s_prod, 1)

            def take_x1_low(n, g):
                dve.wait_ge(s_x1h, n * GROUPS + (g + 1))
                nc.vector.scalar_tensor_tensor(x1_low[g % 2][:, :], x1_ps[:, :], b0[:, 0:1],
                                               x1_high[g % 2][:, :], ALU.add, ALU.subtract)\
                    .then_inc(s_x1l, 1)

            def close_sum(n, t):
                u = n * TILES + t
                v = vec_sum[t % 2]
                dve.wait_ge(s_vstep, u * VSTEPS + 2 * VSTEPS)
                dve.wait_ge(s_pstep, u * STEPS + 2 * STEPS)
                p = pool_sum[t % 2]
                nc.vector.tensor_tensor(p[:, 0:EXTRA_COLS], p[:, 0:EXTRA_COLS], scaled_extra[t % 2][:, :], ALU.add)\
                    .then_inc(s_comb, 1)
                for c in range(2):
                    dve.wait_ge(s_comb, u * COMBS + (c + 1))
                    nc.vector.tensor_tensor(v[:, :], v[:, :], p[:, 2 * S * c:2 * S * (c + 1)],
                                            ALU.add).then_inc(s_comb, 1)
                dve.wait_ge(s_comb, u * COMBS + COMBS)
                dve.wait_ge(s_g, u + 1)
                nc.vector.tensor_tensor(x2[:, :], v[:, 0:S], v[:, S:2 * S], ALU.add).then_inc(s_x2, 1)

            def sum_banks(n, t, behind):
                u = n * TILES + t
                v = [vec_sum[t % 2][:, S * m:S * (m + 1)] for m in range(2)]
                step = 0
                for q in range(HALF):
                    k = 2 * q
                    if k in VEC_BANKS:
                        dve.wait_ge(s_y, u * BANKS + (k + 1) + 1)
                    if q == 0:
                        dve.wait_ge(s_x2, u + 1)
                    for r, i in enumerate(fields_of(k) if k in VEC_BANKS else ()):
                        block_ps = bank[k % RING][:, S * r:S * (r + 1)]
                        x0_i = x0_tokens[t // GROUP_TILES % 2][:, t % GROUP_TILES, i:i + 1]
                        if step >= 2:
                            dve.wait_ge(s_vstep, u * VSTEPS + (VSTEPS + step - 1))
                        if step == 1:
                            ins = nc.vector.tensor_scalar(v[1], block_ps, x0_i, None, ALU.mult)
                        else:
                            ins = nc.vector.scalar_tensor_tensor(
                                v[step % 2], block_ps, x0_i,
                                b1_row[:, :] if step == 0 else v[step % 2], ALU.mult, ALU.add)
                        ins.then_inc(s_vstep, 1)
                        step += 1
                    if q == CLOSE_AT and t >= 1:
                        close_sum(n, t - 1)
                    behind(q)

            def spread_rows(n, t):
                u = n * TILES + t
                if t >= 1:
                    dve.wait_ge(s_g, u - 1 + 1)
                dve.wait_ge(s_mask, 2)
                nc.vector.tensor_tensor(
                    spread[t % 2][:, 0:FIELDS * TILE_ROWS].rearrange("p (i b) -> p i b", b=TILE_ROWS),
                    x0_tokens[t // GROUP_TILES % 2][:, t % GROUP_TILES, :, None].to_broadcast([P, FIELDS, TILE_ROWS]),
                    row_mask[:, None, :].to_broadcast([P, FIELDS, TILE_ROWS]), ALU.mult)\
                    .then_inc(s_spread, 1)

            for c in range(SPLITS):
                split_w1(c)
            for c in range(CHUNKS):
                products(0, 0, c)
            take_x1_low(0, 0)

            def tile_work(n, t, ahead):
                g, tile = t // GROUP_TILES, t % GROUP_TILES
                if tile == 0:
                    dve.wait_ge(s_tokens, n * GROUPS + (g + 1))

                def behind(q):
                    for c in range(CHUNKS):
                        if ahead and PRODUCTS_AT[c] == (tile, q):
                            products(*group_of(n, g + 1), c)
                        if ahead and LOW_BY[c] == VEC and LOW_AT[c] == (tile, q):
                            take_pair_low(dve, *group_of(n, g + 1), c)
                    if (tile, q) == X1_LOW_AT and ahead:
                        take_x1_low(*group_of(n, g + 1))

                sum_banks(n, t, behind)
                spread_rows(n, t)

            def body(n, more):
                for t in range(2, TILES + 2 * more):
                    tile_work(n, t, more or t // GROUP_TILES + 1 < GROUPS)
                if not more:
                    close_sum(n, TILES - 1)

            for t in range(2):
                tile_work(0, t, True)
            blocks(dve, body)


_OUT = ("y", (ROWS, 1), F32)


def kernel(**inputs):
    import concourse.bacc as _bacc
    from concourse.bass_utils import run_bass_kernel_spmd as _run

    w0 = np.asarray(inputs["L0_rec_w0"]).reshape(FIELDS, FIELDS, S)

    def pair_rows(shift, swapped):
        i = np.arange(FIELDS)
        j = (i + shift) % FIELDS
        return w0[j, i] if swapped else w0[i, j]

    def chunks(swapped):
        return np.stack([np.concatenate([pair_rows(CHUNK_SHIFTS * c + r + 1, swapped)
                                         for r in range(CHUNK_SHIFTS)]) for c in range(FULL_CHUNKS)], axis=1)

    tables = [np.asarray(inputs[f"tbl_{f}"]) for f in range(FIELDS)]
    base = np.cumsum([0] + [len(x) for x in tables])
    arrays = {"tables": np.concatenate(tables)}
    ids = np.zeros((BLOCKS * GROUPS, GROUP_ROWS, GATHERS * GATHER_FIELDS), np.int32)
    ids[:, :, 0:FIELDS] = np.asarray(inputs["ids"]).reshape(-1, GROUP_ROWS, FIELDS)
    first = np.zeros_like(ids)
    first[:, :, 0:FIELDS] = base[0:FIELDS]

    def by_partition(x):
        return x.reshape(-1, GROUP_ROWS, GATHERS, GATHER_FIELDS).transpose(3, 1, 0, 2).reshape(P, -1)

    arrays["ids"], arrays["field_base"] = by_partition(ids), by_partition(first)
    arrays["ident"] = np.eye(P, dtype=np.float32)
    arrays["row_mask"] = np.kron(np.eye(TILE_ROWS, dtype=np.float32), np.ones((D, 1), np.float32))
    arrays["w0_pair"], arrays["w0_swap"] = chunks(False), chunks(True)
    arrays["w0_pair_last"] = np.concatenate([pair_rows(SHIFTS - 1, False), pair_rows(0, False)])
    arrays["w0_swap_last"] = pair_rows(SHIFTS - 1, True)
    for w in ("w1", "w2"):
        arrays[w] = np.asarray(inputs[f"L0_rec_{w}"]).reshape(FIELDS, P, S).transpose(1, 0, 2).reshape(P, -1)
    arrays["b0"] = np.asarray(inputs["L0_rec_b0"]).reshape(P, 1)
    arrays["b1"] = np.asarray(inputs["L0_rec_b1"]).reshape(1, S)
    arrays["b2"] = np.asarray(inputs["L0_rec_b2"]).reshape(P, 1)
    top1 = np.asarray(inputs["W_top1"])
    arrays["w_top1"] = top1[0:2 * P].reshape(2, P, TOP1).transpose(1, 0, 2)
    arrays["w_top1c"] = top1[2 * P:]
    arrays["w_top2"] = np.asarray(inputs["W_top2"]).reshape(TOP1 // P, P, TOP2).transpose(1, 0, 2)
    arrays["w_top3"] = np.asarray(inputs["W_top3"]).reshape(TOP2 // P, P).T
    arrays["b_top1"] = np.asarray(inputs["b_top1"]).reshape(TOP1 // P, P).T
    arrays["b_top2"] = np.asarray(inputs["b_top2"]).reshape(TOP2 // P, P).T
    arrays["ctx_t"] = np.asarray(inputs["dense_ctx"]).T
    arrays = {k: np.ascontiguousarray(v) for k, v in arrays.items()}

    nc = _bacc.Bacc("TRN2", target_bir_lowering=False, num_devices=1)
    a = {k: nc.dram_tensor(f"in_{k}", v.shape, mybir.dt.from_np(v.dtype), kind="ExternalInput").ap()
         for k, v in arrays.items()}
    name, shape, dt = _OUT
    out = nc.dram_tensor(name, shape, dt, kind="ExternalOutput").ap()
    dlrm_tower(nc, a, out.rearrange("b a -> a b"))
    r = _run(nc, [{f"in_{k}": v for k, v in arrays.items()}], core_ids=[0])
    return r.results[0][name]
```
